# Optimizing a Trainium2 kernel written in Bass

```python
import numpy as np
import jax
import jax.numpy as jnp

def _softmax(x, axis=-1):
    return jax.nn.softmax(x, axis=axis)

def _gelu(x):
    return jax.nn.gelu(x, approximate=True)

def _silu(x):
    return jax.nn.silu(x)

def _sigmoid(x):
    return jax.nn.sigmoid(x)

def _layernorm(x, axis=-1, eps=1e-05):
    m = jnp.mean(x, axis=axis, keepdims=True)
    v = jnp.var(x, axis=axis, keepdims=True)
    return (x - m) / jnp.sqrt(v + eps)

def _scatter_add(tgt, idx, src, axis=0):
    return tgt.at[idx].add(src)

def _segment_sum(src, seg, n):
    return jax.ops.segment_sum(src, seg, n)
kernel_name = 'mk_prb_d1_jaxref_r4_b65854'

def setup_inputs(seed: int=0):
    np.random.seed(seed)
    _w = jnp.asarray

    def _L0_attn_setup():
        import math
        import jax, jax.numpy as jnp
        import numpy as np
        D_MODEL = 512
        EXPAND = 2
        D_INNER = EXPAND * D_MODEL
        HEADDIM = 64
        NHEADS = D_INNER // HEADDIM
        D_STATE = 128
        CHUNK = 64
        D_CONV = 4
        NGROUPS = 1
        X_PROJ_DIM = D_INNER + NHEADS + 2 * NGROUPS * D_STATE
        BATCH, SEQLEN = (2, 1024)

        def segsum(x):
            T = x.shape[-1]
            cs = jnp.cumsum(x, axis=-1)
            ss = cs[..., :, None] - cs[..., None, :]
            mask = jnp.tril(jnp.ones((T, T), dtype=bool))
            return jnp.where(mask, ss, -jnp.inf)

        def ssd(X, A, B, C, block_len):
            b, l = (X.shape[0], X.shape[1])
            g = B.shape[2]
            h = X.shape[2] // g
            c = l // block_len
            X = X.astype(jnp.float32).reshape(b, c, block_len, g, h, HEADDIM)
            B = B.astype(jnp.float32).reshape(b, c, block_len, g, D_STATE)
            C = C.astype(jnp.float32).reshape(b, c, block_len, g, D_STATE)
            A = A.astype(jnp.float32).reshape(b, c, block_len, g, h)
            A = jnp.transpose(A, (0, 3, 4, 1, 2))
            A_cumsum = jnp.cumsum(A, axis=-1)
            L = jnp.exp(segsum(A))
            Y_diag = jnp.einsum('bclgn,bcsgn,bghcls,bcsghp->bclghp', C, B, L, X)
            decay_states = jnp.exp(A_cumsum[..., -1:] - A_cumsum)
            states = jnp.einsum('bclgn,bghcl,bclghp->bcghpn', B, decay_states, X)
            init = jnp.zeros_like(states[:, :1])
            states = jnp.concatenate([init, states], axis=1)
            chunk_A = jnp.pad(A_cumsum[..., -1], ((0, 0), (0, 0), (0, 0), (1, 0)))
            decay_chunk = jnp.exp(segsum(chunk_A))
            new_states = jnp.einsum('bghzc,bcghpn->bzghpn', decay_chunk, states)
            states, final_state = (new_states[:, :-1], new_states[:, -1])
            state_decay_out = jnp.exp(A_cumsum)
            Y_off = jnp.einsum('bclgn,bcghpn,bghcl->bclghp', C, states, state_decay_out)
            Y = (Y_diag + Y_off).reshape(b, l, g * h, HEADDIM)
            final_state = final_state.reshape(b, g * h, HEADDIM, D_STATE)
            return (Y, final_state)
        key = jax.random.key(seed)
        ks = jax.random.split(key, 8)
        s = 0.02
        u = jax.random.uniform(ks[6], (NHEADS,))
        dt0 = jnp.exp(u * (math.log(0.1) - math.log(0.001)) + math.log(0.001))
        inv_dt = dt0 + jnp.log(-jnp.expm1(-dt0))
        dt_std = NHEADS ** (-0.5)
        return {'x': jax.random.normal(ks[0], (BATCH, SEQLEN, D_MODEL), jnp.float32), 'in_proj_w': jax.random.normal(ks[1], (2 * D_INNER, D_MODEL), jnp.float32) * s, 'conv_w': jax.random.normal(ks[2], (D_INNER, D_CONV), jnp.float32) * s, 'conv_b': jnp.zeros((D_INNER,), jnp.float32), 'x_proj_w': jax.random.normal(ks[3], (X_PROJ_DIM, D_INNER), jnp.float32) * s, 'dt_proj_w': jax.random.uniform(ks[4], (NHEADS, NHEADS), jnp.float32, -dt_std, dt_std), 'dt_proj_b': inv_dt, 'A_log': jnp.log(jnp.arange(1, NHEADS + 1, dtype=jnp.float32)), 'D': jnp.ones((NHEADS,), jnp.float32), 'out_proj_w': jax.random.normal(ks[5], (D_MODEL, D_INNER), jnp.float32) * s}
    _L0_attn_in = _L0_attn_setup()

    def _L0_ffn_setup():
        import jax, jax.numpy as jnp
        import numpy as np
        EPS = 1e-08

        def _quantize(w):
            gamma = jnp.mean(jnp.abs(w))
            return jnp.clip(jnp.round(w / (gamma + EPS)), -1.0, 1.0)

        def _bitlinear(x, w):
            return jnp.matmul(x, _quantize(w).T)
        key = jax.random.key(seed)
        k1, k2, k3, k4 = jax.random.split(key, 4)
        d, h = (512, 1408)
        x = jax.random.normal(k1, (4, 512, d), dtype=jnp.float32)
        w1 = jax.random.normal(k2, (h, d), dtype=jnp.float32)
        w2 = jax.random.normal(k3, (h, d), dtype=jnp.float32)
        w3 = jax.random.normal(k4, (d, h), dtype=jnp.float32)
        return {'x': x, 'w1': w1, 'w2': w2, 'w3': w3}
    _L0_ffn_in = _L0_ffn_setup()
    _d = {'L0_attn_x': _L0_attn_in['x'], 'L0_attn_in_proj_w': _L0_attn_in['in_proj_w'], 'L0_attn_conv_w': _L0_attn_in['conv_w'], 'L0_attn_conv_b': _L0_attn_in['conv_b'], 'L0_attn_x_proj_w': _L0_attn_in['x_proj_w'], 'L0_attn_dt_proj_w': _L0_attn_in['dt_proj_w'], 'L0_attn_dt_proj_b': _L0_attn_in['dt_proj_b'], 'L0_attn_A_log': _L0_attn_in['A_log'], 'L0_attn_D': _L0_attn_in['D'], 'L0_attn_out_proj_w': _L0_attn_in['out_proj_w'], 'L0_ffn_w1': _L0_ffn_in['w1'], 'L0_ffn_w2': _L0_ffn_in['w2'], 'L0_ffn_w3': _L0_ffn_in['w3']}
    _x0 = _d['L0_attn_x']
    _d['L0_attn_x'] = jax.random.normal(jax.random.fold_in(jax.random.key(seed), 1), (2, 2048, 512), dtype=_x0.dtype)
    del _x0
    return _d

def reference(L0_attn_x, L0_attn_in_proj_w, L0_attn_conv_w, L0_attn_conv_b, L0_attn_x_proj_w, L0_attn_dt_proj_w, L0_attn_dt_proj_b, L0_attn_A_log, L0_attn_D, L0_attn_out_proj_w, L0_ffn_w1, L0_ffn_w2, L0_ffn_w3):

    def _L0_attn_ref(x, in_proj_w, conv_w, conv_b, x_proj_w, dt_proj_w, dt_proj_b, A_log, D, out_proj_w):
        import math
        import jax, jax.numpy as jnp
        import numpy as np
        D_MODEL = 512
        EXPAND = 2
        D_INNER = EXPAND * D_MODEL
        HEADDIM = 64
        NHEADS = D_INNER // HEADDIM
        D_STATE = 128
        CHUNK = 64
        D_CONV = 4
        NGROUPS = 1
        X_PROJ_DIM = D_INNER + NHEADS + 2 * NGROUPS * D_STATE
        BATCH, SEQLEN = (2, 1024)

        def segsum(x):
            T = x.shape[-1]
            cs = jnp.cumsum(x, axis=-1)
            ss = cs[..., :, None] - cs[..., None, :]
            mask = jnp.tril(jnp.ones((T, T), dtype=bool))
            return jnp.where(mask, ss, -jnp.inf)

        def ssd(X, A, B, C, block_len):
            b, l = (X.shape[0], X.shape[1])
            g = B.shape[2]
            h = X.shape[2] // g
            c = l // block_len
            X = X.astype(jnp.float32).reshape(b, c, block_len, g, h, HEADDIM)
            B = B.astype(jnp.float32).reshape(b, c, block_len, g, D_STATE)
            C = C.astype(jnp.float32).reshape(b, c, block_len, g, D_STATE)
            A = A.astype(jnp.float32).reshape(b, c, block_len, g, h)
            A = jnp.transpose(A, (0, 3, 4, 1, 2))
            A_cumsum = jnp.cumsum(A, axis=-1)
            L = jnp.exp(segsum(A))
            Y_diag = jnp.einsum('bclgn,bcsgn,bghcls,bcsghp->bclghp', C, B, L, X)
            decay_states = jnp.exp(A_cumsum[..., -1:] - A_cumsum)
            states = jnp.einsum('bclgn,bghcl,bclghp->bcghpn', B, decay_states, X)
            init = jnp.zeros_like(states[:, :1])
            states = jnp.concatenate([init, states], axis=1)
            chunk_A = jnp.pad(A_cumsum[..., -1], ((0, 0), (0, 0), (0, 0), (1, 0)))
            decay_chunk = jnp.exp(segsum(chunk_A))
            new_states = jnp.einsum('bghzc,bcghpn->bzghpn', decay_chunk, states)
            states, final_state = (new_states[:, :-1], new_states[:, -1])
            state_decay_out = jnp.exp(A_cumsum)
            Y_off = jnp.einsum('bclgn,bcghpn,bghcl->bclghp', C, states, state_decay_out)
            Y = (Y_diag + Y_off).reshape(b, l, g * h, HEADDIM)
            final_state = final_state.reshape(b, g * h, HEADDIM, D_STATE)
            return (Y, final_state)
        b, l, _ = x.shape
        xz = x @ in_proj_w.T
        x_branch, z_branch = jnp.split(xz, 2, axis=-1)
        xt = jnp.transpose(x_branch, (0, 2, 1))
        kern = conv_w[:, None, :]
        y = jax.lax.conv_general_dilated(xt, kern, window_strides=(1,), padding=[(D_CONV - 1, 0)], dimension_numbers=('NCH', 'OIH', 'NCH'), feature_group_count=D_INNER)
        x_branch = jnp.transpose(y + conv_b[None, :, None], (0, 2, 1))
        x_branch = jax.nn.silu(x_branch)
        proj = x_branch @ x_proj_w.T
        X = proj[..., :D_INNER].reshape(b, l, NHEADS, HEADDIM)
        dt = proj[..., D_INNER:D_INNER + NHEADS]
        Bm = proj[..., D_INNER + NHEADS:D_INNER + NHEADS + NGROUPS * D_STATE].reshape(b, l, NGROUPS, D_STATE)
        Cm = proj[..., D_INNER + NHEADS + NGROUPS * D_STATE:].reshape(b, l, NGROUPS, D_STATE)
        dt = jax.nn.softplus(dt @ dt_proj_w.T + dt_proj_b)
        A = -jnp.exp(A_log)
        X_scaled = X * dt[..., None]
        A_scaled = A[None, None, :] * dt
        Y, _ = ssd(X_scaled, A_scaled, Bm, Cm, CHUNK)
        Y = Y.astype(x.dtype)
        Y = Y + X * D[None, None, :, None]
        Y = Y.reshape(b, l, D_INNER)
        Y = Y * jax.nn.silu(z_branch)
        return Y @ out_proj_w.T

    def _L0_ffn_ref(x, w1, w2, w3):
        import jax, jax.numpy as jnp
        import numpy as np
        EPS = 1e-08

        def _quantize(w):
            gamma = jnp.mean(jnp.abs(w))
            return jnp.clip(jnp.round(w / (gamma + EPS)), -1.0, 1.0)

        def _bitlinear(x, w):
            return jnp.matmul(x, _quantize(w).T)
        x1 = _bitlinear(x, w1)
        x2 = _bitlinear(x, w2)
        hidden = jax.nn.sigmoid(x1) * x2
        return _bitlinear(hidden, w3)
    x = L0_attn_x
    xn = _layernorm(x, axis=-1)
    x = x + _L0_attn_ref(xn, L0_attn_in_proj_w, L0_attn_conv_w, L0_attn_conv_b, L0_attn_x_proj_w, L0_attn_dt_proj_w, L0_attn_dt_proj_b, L0_attn_A_log, L0_attn_D, L0_attn_out_proj_w) + _L0_ffn_ref(xn, L0_ffn_w1, L0_ffn_w2, L0_ffn_w3)
    return x

_drawn_inputs = setup_inputs


def setup_inputs(seed=0):
    import zlib

    import numpy as np

    out = dict(_drawn_inputs(seed))
    spreads = {'L0_attn_conv_b': (0.0, 0.1), 'L0_attn_D': (1.0, 0.2)}
    factors = {}
    for name, (base, spread) in spreads.items():
        noise = np.random.default_rng([zlib.crc32(name.encode()), seed]).standard_normal(out[name].shape)
        drawn = base * np.exp(spread * noise) if base else spread * noise
        out[name] = jnp.asarray(drawn.astype(out[name].dtype))
    for name, factor in factors.items():
        out[name] = (out[name] * factor).astype(out[name].dtype)
    return out
```

```python
from contextlib import ExitStack

import numpy as np

import concourse.bass as bass
from concourse import mybir

ACT = mybir.ActivationFunctionType
ALU = mybir.AluOpType
F32 = mybir.dt.float32
F16 = mybir.dt.float16
BF16 = mybir.dt.bfloat16
FP8 = mybir.dt.float8e4

P = 128
DMA = 16

XN_SCALE = 2.0 ** 5
W_SCALE = 2.0 ** 8
CONV_SCALE = 2.0 ** 7
S_SCALE = 2.0 * CONV_SCALE
Y_SCALE = 2.0 ** 10
XDT_SCALE = 2.0 ** 10
M_SCALE = 2.0 ** 6
HID_SCALE = 2.0 * XN_SCALE


class Token:

    def __init__(self, stream, section, count, earlier=0):
        self.stream, self.section, self.count, self.earlier = stream, section, count, earlier

    def before(self):
        return Token(self.stream, self.section, self.count, self.earlier + 1)


class Stream:

    def __init__(self, name, setup_sem, block_sem, step=1):
        self.name, self.sem, self.step = name, {"setup": setup_sem, "block": block_sem}, step
        self.counts = {"setup": 0, "loop": 0, "last": 0}

    def mark(self, section):
        self.counts[section] += self.step
        return Token(self, section, self.counts[section])


class Program:

    def __init__(self):
        self.queues = {}
        self.section = "setup"

    def step(self, engine, waits, issue, stream=None, apart=False):
        token = stream.mark(self.section) if stream else None
        flat = []
        for w in waits:
            flat += w if isinstance(w, (list, tuple)) else [w]
        self.queues.setdefault((engine, self.section), []).append(
            (flat, issue, stream, apart))
        return token

    def play(self, engine, handle, section, block):
        reached = {}
        for waits, issue, stream, apart in self.queues.get((engine, section), []):
            waited = False
            for t in waits:
                if t is None:
                    continue
                if callable(t):
                    t = t()
                    if t is None:
                        continue
                    ts = t if isinstance(t, list) else [t]
                else:
                    ts = [t]
                for t in ts:
                    per = t.stream.counts["loop"]
                    if t.section == "setup":
                        sem, level = t.stream.sem["setup"], t.count
                        key = (t.stream.name, "setup")
                        if reached.get(key, 0) >= level:
                            continue
                        reached[key] = level
                        handle.wait_ge(sem, level)
                        continue
                    sem, key = t.stream.sem["block"], (t.stream.name, "block")
                    back = t.earlier if t.section == section else 1
                    level = t.count - back * per
                    if reached.get(key, -10 ** 9) >= level:
                        continue
                    reached[key] = level
                    handle.wait_ge(sem, block * per + (per + level))
                    waited = True
            if apart and waited:
                handle.sem_inc(self.passed, 1)
            made = issue(handle, block)
            if stream is not None:
                made.then_inc(stream.sem["setup" if section == "setup" else "block"], stream.step)


class Slot:

    def __init__(self, program, buffer=None):
        self.program, self.buffer = program, buffer
        self.uses = {"setup": [], "loop": [], "last": []}

    def take(self):
        section = self.program.section
        uses = self.uses[section]
        uses.append([])
        n = len(uses) - 1
        if n:
            assert uses[n - 1], "taken before its last user's readers are known"
            return list(uses[n - 1])
        if section == "setup":
            return []
        last = self.uses["loop"]
        if section == "last":
            return list(last[-1])
        start = self.uses["setup"][-1] if self.uses["setup"] else []
        return [*start, lambda: [t.before() for t in last[-1]]]

    def done(self, *tokens):
        self.uses[self.program.section][-1] += tokens


def mamba_ffn_block(nc, x, w_in, conv_w, conv_b, w_x, w_xdt, w_dt, dt_bias, a_log, d_skip, w_out,
                    w_ffn, ident, mask_neg, upper, cs_lhs, cs_rhs, out):
    batches, seqlen, dm = x.shape
    di = w_in.shape[1] // 2
    heads = w_dt.shape[0]
    hd = di // heads
    ns = (w_x.shape[1] - di) // 2
    fh = (w_ffn.shape[1]) // (3 * dm) * P
    tb = 512
    nb = batches * seqlen // tb
    span = tb // batches
    chunks = tb // P
    kd, ki, kf = dm // P, di // P, fh // P
    taps = conv_w.shape[2]
    halo = taps - 1
    half = 512
    halves = di // half
    hph = half // hd
    hpg = half // P
    assert batches == 2 and ns == P and chunks == 4 and dm == half and heads == 16

    pr = Program()
    ctx = ExitStack()
    with ctx:
        def sem(name):
            return ctx.enter_context(nc.semaphore(name))

        pr.passed = sem("passed")

        def stream(name, step=1):
            return Stream(name, sem(name + "_setup"), sem(name + "_blocks"), step)

        def sb(name, shape, dt=F32, where=ctx):
            return where.enter_context(nc.sbuf_tensor(name, shape, dt))

        pe, act, dve, pool = (stream(n) for n in ("pe", "act", "dve", "pool"))
        st_x = [stream(f"x_in{n}", DMA) for n in range(4)]
        st_res = [stream(f"residual{c}", DMA) for c in range(chunks)]
        st_out = [stream(f"stored{c}", DMA) for c in range(chunks)]
        st_rows = stream("cs_rows", DMA)
        st_small = stream("small", DMA)
        streams = [pe, act, dve, pool, *st_x, *st_res, *st_out, st_rows]

        def on_pe(waits, issue, mark=True, apart=False):
            return pr.step("tensor", waits, issue, pe if mark else None, apart)

        def on_act(waits, issue):
            return pr.step("scalar", waits, issue, act)

        def on_dve(waits, issue, apart=False):
            return pr.step("vector", waits, issue, dve, apart)

        def on_pool(waits, issue, apart=False):
            return pr.step("gpsimd", waits, issue, pool, apart)

        def load(waits, issue, st):
            return pr.step("sync", waits, issue, st)

        win = [sb(f"win_{p}", [P, kd, 2 * di], F16) for p in ("hi", "lo")]
        wx = [sb(f"wx_{p}", [P, ki, w_x.shape[1]], F16) for p in ("hi", "lo")]
        wo = [sb(f"wo_{p}", [P, ki, dm], F16) for p in ("hi", "lo")]
        q12 = sb("q12", [P, 2, kd, fh], FP8)
        q3 = sb("q3", [P, kf, dm], FP8)
        idn = sb("idn", [P, P])
        idb = sb("idb", [P, P], BF16)
        neg = sb("neg", [P, half], BF16)
        upp = sb("upp", [P, P])
        ones = sb("ones", [P, P])
        lhs_cs = sb("lhs_cs", [P, chunks, P], BF16)
        rhs_cs = sb("rhs_cs", [P, heads * P], BF16)
        cw = sb("cw", [P, ki, taps])
        cws = sb("cws", [P, ki])
        cb = sb("cb", [P, ki])
        w2 = [sb(f"w2_{p}", [P, ki, heads], F16) for p in ("hi", "lo")]
        dtb = sb("dtb", [P, heads])
        na = sb("na", [P, heads])
        dsk = sb("dsk", [P, heads])
        mhalf = sb("mhalf", [P, chunks])
        thr = sb("thr", [P, 3])
        nthr = sb("nthr", [P, 3])
        state = [sb(f"state{b}", [P, di]) for b in range(batches)]
        hal = sb("hal", [P, ki, batches, halo])

        banks = [Slot(pr, ctx.enter_context(nc.psum_tensor(f"bank{n}", [P, half], F32)))
                 for n in range(8)]

        early = ExitStack()
        stg_n = 2
        stage = [Slot(pr, sb(f"stage{n}", [P, 2 * di], where=early)) for n in range(stg_n)]
        st_stage = [stream(f"stage{n}", DMA) for n in range(stg_n)]
        ffn = [sb(f"ffn{n}", [P, kd * fh], where=early) for n in range(3)]
        st_ffn = [stream(f"ffn{n}", DMA) for n in range(3)]
        junk = Slot(pr, sb("junk", [P, fh], BF16, where=early))
        below = [Slot(pr, sb(f"below{n}", [P, fh], BF16, where=early)) for n in range(2)]
        asum = sb("asum", [P, 3, kd], where=early)
        tsum = sb("tsum", [P, 3], where=early)
        gam = sb("gam", [P, 3], where=early)

        wdt = sb("wdt", [heads, heads], where=early)
        wxdt = sb("wxdt", [heads, di], where=early)
        small = None
        for dst, src in ((idn, ident), (neg, mask_neg), (upp, upper), (lhs_cs, cs_lhs),
                         (rhs_cs, cs_rhs), (cw, conv_w), (cb, conv_b), (wdt, w_dt),
                         (wxdt, w_xdt)):
            small = load([], lambda e, _, dst=dst, src=src: e.dma_start(dst[:], src), st_small)
        for dst, src in ((dtb, dt_bias), (na, a_log), (dsk, d_skip)):
            small = load([], lambda e, _, dst=dst, src=src: e.dma_start(
                dst[:], src.unsqueeze(0).to_broadcast([P, heads])), st_small)

        pieces = []
        for k in range(kd):
            pieces.append((w_in[k * P:(k + 1) * P, :], 2 * di, [w[:, k, :] for w in win]))
        for k in range(ki):
            pieces.append((w_x[k * P:(k + 1) * P, :], w_x.shape[1], [w[:, k, :] for w in wx]))
        for k in range(ki):
            pieces.append((w_out[k * P:(k + 1) * P, :], dm, [w[:, k, :] for w in wo]))
        for n, (src, cols, (hi, lo)) in enumerate(pieces):
            s = stage[n % stg_n]
            buf = s.buffer
            free = s.take()
            landed = load(free, lambda e, _, buf=buf, cols=cols, src=src: e.dma_start(
                buf[:, 0:cols], src), st_stage[n % stg_n])
            t_hi = on_act([landed], lambda e, _, hi=hi, buf=buf, cols=cols: e.activation(
                hi, buf[:, 0:cols], ACT.Copy, scale=W_SCALE))
            t_lo = on_dve([landed, t_hi], lambda e, _, hi=hi, lo=lo, buf=buf, cols=cols:
                          e.scalar_tensor_tensor(out=lo, in0=buf[:, 0:cols], scalar=W_SCALE,
                                                 in1=hi, op0=ALU.mult, op1=ALU.subtract))
            s.done(t_hi, t_lo)
            if n < 3:
                j = n
                st = load([], lambda e, _, j=j: e.dma_start(
                    ffn[j][:], w_ffn[:, j * kd * fh:(j + 1) * kd * fh]), st_ffn[j])
                ffn_in = [st] if n == 0 else ffn_in + [st]

        t_one = on_pool([], lambda e, _: e.memset(ones[:], 1.0))
        t_clear = [on_pool([], lambda e, _, b=b: e.memset(state[b][:], 0.0)) for b in range(batches)]
        t_clear.append(on_pool([], lambda e, _: e.memset(hal[:], 0.0)))
        t_clear.append(on_pool([], lambda e, _: e.memset(mhalf[:], -0.5)))

        free = banks[1].take()
        for k in range(ki):
            t_w2 = on_pe([small, free], lambda e, _, k=k: e.matmul(
                banks[1].buffer[:, k * heads:(k + 1) * heads], wxdt[:, k * P:(k + 1) * P], wdt[:],
                start=True, stop=True))
        flat = [w[:].rearrange("p k h -> p (k h)") for w in w2]
        t_hi = on_act([t_w2], lambda e, _: e.activation(
            flat[0], banks[1].buffer[:, 0:ki * heads], ACT.Copy, scale=W_SCALE))
        t_w2 = on_dve([t_hi], lambda e, _: e.scalar_tensor_tensor(
            out=flat[1], in0=banks[1].buffer[:, 0:ki * heads], scalar=W_SCALE, in1=flat[0],
            op0=ALU.mult, op1=ALU.subtract))
        banks[1].done(t_hi, t_w2)

        for j in range(3):
            for k in range(kd):
                free = junk.take()
                t_abs = on_act([ffn_in[j], free], lambda e, _, j=j, k=k: e.activation(
                    junk.buffer[:], ffn[j][:, k * fh:(k + 1) * fh], ACT.Abs,
                    accum_out=asum[:, j, k:k + 1]))
                junk.done(t_abs)
        t_sum = on_dve([t_abs], lambda e, _: e.reduce_sum(tsum[:], asum[:], mybir.AxisListType.X))
        free = banks[0].take()
        t_tot = on_pe([t_sum, t_one], lambda e, _: e.matmul(
            banks[0].buffer[:, 0:3], ones[:], tsum[:], start=True, stop=True))
        t_gam = on_dve([t_tot], lambda e, _: e.tensor_scalar(
            gam[:], banks[0].buffer[:, 0:3], 1.0 / (dm * fh), 1e-8, ALU.mult, ALU.add))
        banks[0].done(t_gam)
        t_thr = on_dve([t_gam], lambda e, _: e.tensor_scalar(thr[:], gam[:], 0.5, None, ALU.mult))
        t_thr = on_dve([t_gam], lambda e, _: e.tensor_scalar(nthr[:], gam[:], -0.5, None, ALU.mult))
        for j in range(3):
            for k in range(kd):
                w = ffn[j][:, k * fh:(k + 1) * fh]
                q = q12[:, j, k, :] if j < 2 else q3[:].rearrange("p k n -> p (k n)")[:, k * fh:(k + 1) * fh]
                bl = below[k % 2]
                free = bl.take()
                t_b = on_dve([t_thr, free], lambda e, _, w=w, j=j, bl=bl: e.tensor_scalar(
                    bl.buffer[:], w, nthr[:, j:j + 1], None, ALU.is_lt))
                t_q = on_dve([t_b], lambda e, _, w=w, j=j, q=q, bl=bl: e.scalar_tensor_tensor(
                    out=q, in0=w, scalar=thr[:, j:j + 1], in1=bl.buffer[:], op0=ALU.is_gt,
                    op1=ALU.subtract, saturate=False))
                bl.done(t_q)
        t_exp = on_act([small], lambda e, _: e.activation(na[:], na[:], ACT.Exp))
        on_dve([t_exp], lambda e, _: e.tensor_scalar(na[:], na[:], -1.0, None, ALU.mult))
        on_dve([small], lambda e, _: e.tensor_copy(idb[:], idn[:]))
        t_cws = on_dve([small], lambda e, _: e.tensor_scalar(
            cws[:], cw[:, :, taps - 1], CONV_SCALE / (XN_SCALE * W_SCALE), None, ALU.mult))
        t_cw = on_dve([small, t_cws], lambda e, _: e.tensor_scalar(cw[:], cw[:], CONV_SCALE, None, ALU.mult))
        t_cb = on_dve([small], lambda e, _: e.tensor_scalar(cb[:], cb[:], CONV_SCALE, None, ALU.mult))
        set_up = [t_q, t_cb, t_lo, t_exp, t_clear[-1]]
        early.close()

        stats = sb("stats", [P, chunks, 6])
        mv = sb("mv", [P, chunks, 2])
        rstd = sb("rstd", [P, chunks])
        rstd_s = Slot(pr)
        xt = [sb(f"xt_{p}", [P, kd, tb], F16) for p in ("hi", "lo")]
        raw = [Slot(pr, sb(f"raw{n}", [P, batches, halo + span])) for n in range(2)]
        acc = [Slot(pr, sb(f"acc{n}", [P, tb])) for n in range(2)]
        tnh = [Slot(pr, sb(f"tnh{n}", [P, tb])) for n in range(2)]
        full = [Slot(pr, sb(f"full{n}", [P, tb])) for n in range(2)]
        arena = sb("arena", [P, 2 * kf * tb], F16)
        s_parts = [arena[:, p * ki * tb:(p + 1) * ki * tb].rearrange("p (k t) -> p k t", k=ki)
                   for p in range(2)]
        after_s = 2 * ki * tb
        bt = arena[:, after_s:after_s + 2 * tb].bitcast(F32)
        ct = arena[:, after_s + 2 * tb:after_s + 4 * tb].bitcast(F32)
        btok = arena[:, after_s + 4 * tb:after_s + 6 * tb].bitcast(F32)
        hid = arena[:].rearrange("p (k q t) -> p k q t", k=kf, q=2)
        arena_s, arena_b = Slot(pr), Slot(pr)
        gt = sb("gt", [P, chunks, P])
        gt_s = Slot(pr)
        sml = {n: sb(n, [P, chunks, heads]) for n in
               ("dtv", "dab", "du", "dz", "dq", "dp", "dt", "av", "cs", "ecs", "dst", "dec")}
        ap3 = sb("ap3", [P, chunks, 96])
        cst = sb("cst", [96, tb])
        csp = sb("csp", [96, tb], BF16)
        small_s = Slot(pr)
        xs = [Slot(pr, sb(f"xs{n}", [P, half])) for n in range(2)]
        xdt = Slot(pr, sb("xdt", [P, half]))
        xdp = [sb(f"xdt_{p}", [P, half], F16) for p in ("hi", "lo")]
        xdp_s = Slot(pr)
        xst = Slot(pr, sb("xst", [P, half]))
        yac = [Slot(pr, sb(f"yac{n}", [P, half])) for n in range(2)]
        gate = [Slot(pr, sb(f"gate{n}", [P, half])) for n in range(2)]
        xin = [*yac, *gate]
        edc = [Slot(pr, sb(f"edc{n}", [P, hpg * P])) for n in range(2)]
        mdc = [Slot(pr, [sb(f"mdc{n}_{p}", [P, hpg * P], F16) for p in ("hi", "lo")]) for n in range(4)]
        yt = [sb(f"yt_{p}", [P, ki, P], F16) for p in ("hi", "lo")]
        yt_s = Slot(pr)
        res = [Slot(pr, sb(f"res{c}", [P, dm])) for c in range(chunks)]

        def heads_over(v, h0, n, width):
            return v[:, h0:h0 + n].unsqueeze(2).to_broadcast([P, n, width])

        def by_head(v, width):
            return v.rearrange("p (h d) -> p h d", d=width)

        def rows(dram, c, block):
            b, at = c // (chunks // batches), (c % (chunks // batches)) * P
            if isinstance(block, int):
                return dram[b, block * span + at:block * span + at + P, :]
            return dram[b, bass.ds(block * span + at, P), :]

        def split_passes(a, b):
            return [(a[0], b[0]), (a[0], b[1]), (a[1], b[0])]

        def norm(shift):
            x_tok, seen = [], {}

            def statistics(c):
                if c == 0:
                    seen["free"] = rstd_s.take()
                s = xin[c]
                free = s.take()
                landed = load([free], lambda e, blk: e.dma_start(
                    s.buffer[:], rows(x, c, blk + shift)), st_x[c])
                t = on_dve([landed, seen["free"]], lambda e, _: e.bn_stats(stats[:, c, :], s.buffer[:]))
                seen["mv", c] = on_dve([t], lambda e, _: e.bn_aggr(mv[:, c, :], stats[:, c, :]), apart=True)

            def root():
                t = on_dve([seen["mv", chunks - 1]], lambda e, _: e.tensor_scalar(
                    rstd[:], mv[:, :, 1], 1e-5, None, ALU.add))
                t = on_pool([t], lambda e, _: e.tensor_tensor(rstd[:], rstd[:], mhalf[:], ALU.pow))
                seen["root"] = on_dve([t], lambda e, _: e.tensor_scalar(
                    rstd[:], rstd[:], XN_SCALE, None, ALU.mult))

            def normalise(c):
                s = xin[c]
                t = on_dve([seen["root"]], lambda e, _: e.tensor_scalar(
                    s.buffer[:], s.buffer[:], mv[:, c, 0:1], rstd[:, c:c + 1], ALU.subtract, ALU.mult))
                x_tok.append(t)
                if c == chunks - 1:
                    rstd_s.done(t)

            steps = [lambda c=c: statistics(c) for c in range(chunks)]
            steps += [root] + [lambda c=c: normalise(c) for c in range(chunks)]
            return steps, x_tok

        def turn(x_tok, xt_free):
            for k in range(kd):
                bk = banks[4 + k]
                free = bk.take()
                for c in range(chunks):
                    t_t = on_pe([free, x_tok[c]], lambda e, _, k=k, c=c, bk=bk: e.transpose(
                        bk.buffer[:, c * P:(c + 1) * P], xin[c].buffer[:, k * P:(k + 1) * P], idn[:]),
                        mark=(c == chunks - 1))
                t_hi = on_act([t_t, xt_free], lambda e, _, k=k, bk=bk: e.copy(xt[0][:, k, :], bk.buffer[:]))
                t_lo = on_dve([t_hi, xt_free], lambda e, _, k=k, bk=bk: e.tensor_tensor(
                    xt[1][:, k, :], bk.buffer[:], xt[0][:, k, :], ALU.subtract))
                bk.done(t_hi, t_lo)
            for s in xin:
                s.done(t_t)
            return t_lo

        def body(last):
            xt_ready = [xt_made["loop"]] if last else [xt_first, lambda: [xt_made["loop"].before()]]
            s_free, b_free = arena_s.take(), arena_b.take()
            s_ready = []
            conv = {}

            def in_proj(m):
                bk = banks[4 + m % 4]
                free = bk.take()
                n = 0
                for k in range(kd):
                    for a, b in split_passes(win, xt):
                        n += 1
                        t_mm = on_pe([free, xt_ready] if n == 1 else [],
                                     lambda e, _, k=k, a=a, b=b, n=n: e.matmul(
                                         bk.buffer[:], a[:, k, m * P:(m + 1) * P], b[:, k, :],
                                         start=(n == 1), stop=(n == 3 * kd)),
                                     mark=(n == 3 * kd))
                r, a_, tp = raw[m % 2], acc[m % 2], (xdt, xst)[m % 2]
                r_free, a_free, p_free = r.take(), a_.take(), tp.take()
                ps3 = bk.buffer[:].rearrange("p (b t) -> p b t", b=batches)
                acc3 = a_.buffer[:].rearrange("p (b t) -> p b t", b=batches)
                tp3 = tp.buffer[:].rearrange("p (b t) -> p b t", b=batches)
                t_raw = on_act([t_mm, r_free], lambda e, _: e.activation(
                    r.buffer[:, :, halo:], ps3, ACT.Copy, scale=1.0 / (XN_SCALE * W_SCALE)))
                t_acc = on_act([a_free], lambda e, _: e.activation(
                    a_.buffer[:], bk.buffer[:], ACT.Identity, scale=cws[:, m:m + 1], bias=cb[:, m:m + 1]))
                bk.done(t_acc)
                t_h = on_pool([r_free], lambda e, _: e.tensor_copy(
                    r.buffer[:, :, 0:halo], hal[:, m, :, :]), apart=True)
                t_h2 = on_pool([t_h, t_raw], lambda e, _: e.tensor_copy(
                    hal[:, m, :, :], r.buffer[:, :, span:span + halo]), apart=True)
                t_tap = on_act([t_h, t_raw, p_free], lambda e, _: e.mul(
                    tp3, r.buffer[:, :, halo - 1:halo - 1 + span], cw[:, m, halo - 1:halo]))
                t_add = on_pool([t_acc, t_tap], lambda e, _: e.tensor_tensor(
                    a_.buffer[:], a_.buffer[:], tp.buffer[:], ALU.add))
                tp.done(t_add)
                t_c = t_add
                for j in range(halo - 1):
                    t_c = on_dve([t_c, t_h2], lambda e, _, j=j: e.scalar_tensor_tensor(
                        out=acc3, in0=r.buffer[:, :, j:j + span],
                        scalar=cw[:, m, j:j + 1], in1=acc3, op0=ALU.mult, op1=ALU.add))
                r.done(t_c, t_h2, t_tap)
                conv[m] = (a_, t_c)

            def silu(m):
                a_, t_c = conv[m]
                th, fl = tnh[m % 2], full[m % 2]
                th_free, fl_free = th.take(), fl.take()
                t_th = on_act([t_c, th_free], lambda e, _: e.activation(
                    th.buffer[:], a_.buffer[:], ACT.Tanh, scale=0.5 / CONV_SCALE))
                t_f = on_dve([t_th, fl_free], lambda e, _: e.scalar_tensor_tensor(
                    out=fl.buffer[:], in0=th.buffer[:], scalar=1.0, in1=a_.buffer[:],
                    op0=ALU.add, op1=ALU.mult))
                a_.done(t_f)
                th.done(t_f)
                t_hi = on_pool([t_f, s_free], lambda e, _: e.tensor_scalar(
                    s_parts[0][:, m, :], fl.buffer[:], 1.0, 0.0, ALU.mult, ALU.add), apart=True)
                conv[m] = (fl, t_hi)

            def silu_rest(m):
                fl, t_hi = conv[m]
                t_lo = on_dve([t_hi, s_free], lambda e, _: e.tensor_tensor(
                    s_parts[1][:, m, :], fl.buffer[:], s_parts[0][:, m, :], ALU.subtract))
                fl.done(t_lo)
                s_ready.append(t_lo)

            for m in range(ki + 2):
                if m < ki:
                    in_proj(m)
                if 1 <= m <= ki:
                    silu(m - 1)
                if m >= 2:
                    silu_rest(m - 2)

            order = [0, 2, 1, 3]
            units = [(c, hf) for c in order for hf in range(halves)]
            gates, xes = {}, {}

            def project_z(u):
                c, hf = units[u]
                bz = banks[1]
                free = bz.take()
                n = 0
                for k in range(kd):
                    for a, b in split_passes(xt, win):
                        n += 1
                        t_z = on_pe([free], lambda e, _, k=k, a=a, b=b, n=n: e.matmul(
                            bz.buffer[:], a[:, k, c * P:(c + 1) * P],
                            b[:, k, di + hf * half:di + (hf + 1) * half],
                            start=(n == 1), stop=(n == 3 * kd)), mark=(n == 3 * kd))
                g_, th = gate[u % 2], tnh[u % 2]
                g_free, th_free = g_.take(), th.take()
                t_th = on_act([t_z, th_free], lambda e, _: e.activation(
                    th.buffer[:], bz.buffer[:], ACT.Tanh, scale=0.5 / (XN_SCALE * W_SCALE)))
                t_gz = on_dve([t_th, g_free], lambda e, _: e.scalar_tensor_tensor(
                    out=g_.buffer[:], in0=th.buffer[:], scalar=1.0, in1=bz.buffer[:],
                    op0=ALU.add, op1=ALU.mult))
                bz.done(t_gz)
                th.done(t_gz)
                gates[u] = (g_, t_gz)

            project_z(0)
            project_z(1)

            def project(bk, col, width):
                free = bk.take()
                n = 0
                for k in range(ki):
                    for a, b in split_passes(wx, s_parts):
                        n += 1
                        t = on_pe([free, s_ready[k]], lambda e, _, k=k, a=a, b=b, n=n: e.matmul(
                            bk.buffer[0:width, :], a[:, k, col:col + width], b[:, k, :],
                            start=(n == 1), stop=(n == 3 * ki)), mark=(n == 3 * ki))
                return t

            unscale = 1.0 / (S_SCALE * W_SCALE)
            sm_free = small_s.take()
            free = banks[2].take()
            for c in range(chunks):
                n = 0
                for k in range(ki):
                    for a, b in split_passes(s_parts, w2):
                        n += 1
                        t_dp = on_pe([free, s_ready[k]], lambda e, _, c=c, k=k, a=a, b=b, n=n: e.matmul(
                            banks[2].buffer[:, c * heads:(c + 1) * heads], a[:, k, c * P:(c + 1) * P],
                            b[:, k, :], start=(n == 1), stop=(n == 3 * ki)),
                            mark=(c == chunks - 1 and n == 3 * ki))
            t_b = project(banks[3], di, ns)
            t_bt = on_act([t_b, b_free], lambda e, _: e.mul(bt, banks[3].buffer[:], unscale))
            banks[3].done(t_bt)
            v = {n: t[:].rearrange("p c h -> p (c h)") for n, t in sml.items()}
            t1 = on_dve([t_dp, sm_free], lambda e, _: e.scalar_tensor_tensor(
                out=sml["dtv"][:], scalar=unscale, op0=ALU.mult, op1=ALU.add,
                in0=banks[2].buffer[:, 0:chunks * heads].rearrange("p (c h) -> p c h", h=heads),
                in1=dtb[:].unsqueeze(1).to_broadcast([P, chunks, heads])))
            banks[2].done(t1)
            t2 = on_dve([t1], lambda e, _: e.scalar_tensor_tensor(
                out=v["dab"], in0=v["dtv"], scalar=-1.0, in1=v["dtv"], op0=ALU.mult, op1=ALU.max))
            t3 = on_act([t2], lambda e, _: e.activation(v["du"], v["dab"], ACT.Exp, scale=-1.0))
            t4 = on_dve([t3], lambda e, _: e.tensor_scalar(v["dab"], v["du"], 2.0, None, ALU.add))
            t4 = on_dve([t4], lambda e, _: e.reciprocal(v["dz"], v["dab"]))
            t4 = on_dve([t4], lambda e, _: e.tensor_tensor(v["dz"], v["dz"], v["du"], ALU.mult))
            t4 = on_dve([t4], lambda e, _: e.tensor_tensor(v["dq"], v["dz"], v["dz"], ALU.mult))
            t4 = on_dve([t4], lambda e, _: e.tensor_scalar(v["dp"], v["dq"], 1.0 / 17, None, ALU.mult))
            for odd in range(15, 1, -2):
                t4 = on_dve([t4], lambda e, _, odd=odd: e.scalar_tensor_tensor(
                    out=v["dp"], in0=v["dp"], scalar=1.0 / odd, in1=v["dq"], op0=ALU.add, op1=ALU.mult))
            t4 = on_dve([t4], lambda e, _: e.scalar_tensor_tensor(
                out=v["dp"], in0=v["dp"], scalar=1.0, in1=v["dz"], op0=ALU.add, op1=ALU.mult))
            t4 = on_dve([t4], lambda e, _: e.tensor_scalar(v["dab"], v["dtv"], 0.0, None, ALU.max))
            t_dtf = on_dve([t4], lambda e, _: e.scalar_tensor_tensor(
                out=v["dt"], in0=v["dp"], scalar=2.0, in1=v["dab"], op0=ALU.mult, op1=ALU.add))
            t_av = on_dve([t_dtf], lambda e, _: e.tensor_tensor(
                sml["av"][:], sml["dt"][:], na[:].unsqueeze(1).to_broadcast([P, chunks, heads]), ALU.mult))
            for j in range(3):
                t_ap = on_dve([t_av, sm_free], lambda e, _, j=j: e.tensor_copy(
                    ap3[:, :, 32 * j:32 * j + heads], sml["av"][:]))
            t_c = project(banks[4], di + ns, ns)
            t_ct = on_act([t_c], lambda e, _: e.mul(ct, banks[4].buffer[:], unscale))
            banks[4].done(t_ct)
            free = banks[5].take()
            w = chunks * heads
            on_pe([free, t_av], lambda e, _: e.matmul(
                banks[5].buffer[:, 0:w], upp[:], v["av"], start=True, stop=True), mark=False)
            t_cs = on_pe([], lambda e, _: e.matmul(
                banks[5].buffer[:, w:2 * w], ones[:], v["av"], start=True, stop=True))
            free = banks[6].take()
            for c in range(chunks):
                t_cst = on_pe([free, t_ap], lambda e, _, c=c: e.matmul(
                    banks[6].buffer[0:96, c * P:(c + 1) * P], ap3[:, c, :], upp[:],
                    start=True, stop=True), mark=(c == chunks - 1))
            t_e1 = on_act([t_cs, sm_free], lambda e, _: e.activation(v["ecs"], banks[5].buffer[:, 0:w], ACT.Exp))
            t_e2 = on_act([], lambda e, _: e.activation(v["dec"], banks[5].buffer[:, w:2 * w], ACT.Exp))
            t_e3 = on_dve([t_cs, t_e2, sm_free], lambda e, _: e.tensor_copy(v["cs"], banks[5].buffer[:, 0:w]))
            t_e3 = on_dve([t_e3], lambda e, _: e.tensor_tensor(
                v["cs"], banks[5].buffer[:, w:2 * w], v["cs"], ALU.subtract))
            banks[5].done(t_e1, t_e2, t_e3)
            t_e3 = on_act([t_e3], lambda e, _: e.activation(v["dst"], v["cs"], ACT.Exp))
            decays = [t_e1, t_e2, t_e3, t_dtf]
            q0, q1, q2 = (slice(32 * j, 32 * j + 32) for j in range(3))
            t_f = on_dve([t_cst, sm_free], lambda e, _: e.tensor_copy(cst[:], banks[6].buffer[0:96, :]))
            banks[6].done(t_f)
            t_p = on_dve([t_f], lambda e, _: e.tensor_copy(csp[:], cst[:]))
            t_f = on_dve([t_p], lambda e, _: e.tensor_tensor(cst[q1, :], cst[q1, :], csp[q1, :], ALU.subtract))
            t_f = on_dve([t_f], lambda e, _: e.tensor_tensor(cst[q2, :], cst[q2, :], csp[q2, :], ALU.subtract))
            t_p = on_dve([t_f], lambda e, _: e.tensor_copy(csp[q1, :], cst[q1, :]))
            t_p = on_dve([t_p], lambda e, _: e.tensor_copy(csp[q2, :], cst[q2, :]))
            t_f = on_dve([t_p], lambda e, _: e.tensor_tensor(cst[q2, :], cst[q2, :], csp[q2, :], ALU.subtract))
            t_p = on_dve([t_f], lambda e, _: e.tensor_copy(csp[q2, :], cst[q2, :]))
            t_l = on_dve([t_p, sm_free], lambda e, _: e.tensor_scalar(
                lhs_cs[0:96, :, :].rearrange("p c t -> p (c t)"), csp[:], -1.0, None, ALU.mult))
            for j in range(3):
                for c in range(chunks):
                    r0 = 96 + 3 * c + j
                    t_r = load([t_p, sm_free], lambda e, _, j=j, c=c, r0=r0: e.dma_start(
                        rhs_cs[r0:r0 + 1, :], csp[32 * j:32 * j + heads, c * P:(c + 1) * P]), st_rows)
            args_ready = [t_l, t_r]

            free = banks[2].take()
            for c in range(chunks):
                t_t = on_pe([t_bt, free], lambda e, _, c=c: e.transpose(
                    banks[2].buffer[:, c * P:(c + 1) * P], bt[:, c * P:(c + 1) * P], idn[:]),
                    mark=(c == chunks - 1))
            t_bk = on_act([t_t], lambda e, _: e.copy(btok, banks[2].buffer[:]))
            banks[2].done(t_bk)
            free = banks[3].take()
            for c in range(chunks):
                t_g = on_pe([t_ct, t_bt, free], lambda e, _, c=c: e.matmul(
                    banks[3].buffer[:, c * P:(c + 1) * P], bt[:, c * P:(c + 1) * P],
                    ct[:, c * P:(c + 1) * P], start=True, stop=True), mark=(c == chunks - 1))
            g_free = gt_s.take()
            t_gt = on_act([t_g, g_free], lambda e, _: e.copy(gt[:].rearrange("p c t -> p (c t)"), banks[3].buffer[:]))
            banks[3].done(t_gt)

            def project_x(u):
                c, hf = units[u]
                bx = banks[0]
                free = bx.take()
                n = 0
                for k in range(ki):
                    for a, b in split_passes(s_parts, wx):
                        n += 1
                        t_x = on_pe([free, s_ready[k]], lambda e, _, k=k, a=a, b=b, n=n: e.matmul(
                            bx.buffer[:], a[:, k, c * P:(c + 1) * P], b[:, k, hf * half:(hf + 1) * half],
                            start=(n == 1), stop=(n == 3 * ki)), mark=(n == 3 * ki))
                x_ = xs[u % 2]
                x_free = x_.take()
                t_xs = on_act([t_x, x_free], lambda e, _: e.mul(x_.buffer[:], bx.buffer[:], unscale))
                bx.done(t_xs)
                h0 = hf * hph
                d_free, e_free, p_free = xdt.take(), xst.take(), xdp_s.take()
                t_xd = on_dve([t_xs, t_dtf, d_free], lambda e, _: e.tensor_tensor(
                    by_head(xdt.buffer[:], hd), by_head(x_.buffer[:], hd),
                    heads_over(sml["dt"][:, c, :], h0, hph, hd), ALU.mult))
                t_sk = on_pool([t_xd], lambda e, _: e.tensor_tensor(
                    by_head(x_.buffer[:], hd), by_head(x_.buffer[:], hd),
                    heads_over(dsk[:], h0, hph, hd), ALU.mult))
                t_xe = on_pool([t_xd, decays, e_free], lambda e, _: e.tensor_tensor(
                    by_head(xst.buffer[:], hd), by_head(xdt.buffer[:], hd),
                    heads_over(sml["dst"][:, c, :], h0, hph, hd), ALU.mult))
                t_hi = on_act([t_xd, p_free], lambda e, _: e.mul(xdp[0][:], xdt.buffer[:], XDT_SCALE))
                t_lo = on_dve([t_hi, p_free], lambda e, _: e.scalar_tensor_tensor(
                    out=xdp[1][:], in0=xdt.buffer[:], scalar=XDT_SCALE, in1=xdp[0][:],
                    op0=ALU.mult, op1=ALU.subtract))
                xdt.done(t_xe, t_lo)
                xes[u] = (x_, t_x, t_sk, t_xe, t_lo)

            def decay(u):
                c, hf = units[u]
                out_ = []
                for g in range(hph // hpg):
                    h0 = hf * hph + g * hpg
                    bk, ed, md = banks[2 + g], edc[g], mdc[2 * (u % 2) + g]
                    free = bk.take()
                    on_pe([free, args_ready], lambda e, _, h0=h0, bk=bk: e.matmul(
                        bk.buffer[:], lhs_cs[:, c, :], rhs_cs[:, h0 * P:(h0 + hpg) * P],
                        start=True, stop=False), mark=False)
                    t_a = on_pe([], lambda e, _, bk=bk: e.matmul(
                        bk.buffer[:], idb[:], neg[:], start=False, stop=True))
                    e_free, m_free = ed.take(), md.take()
                    t_e = on_act([t_a, e_free], lambda e, _, bk=bk, ed=ed: e.activation(
                        ed.buffer[:], bk.buffer[:], ACT.Exp))
                    bk.done(t_e)
                    t_m = on_dve([t_e, t_gt], lambda e, _, ed=ed: e.tensor_tensor(
                        by_head(ed.buffer[:], P), by_head(ed.buffer[:], P),
                        gt[:, c, :].unsqueeze(1).to_broadcast([P, hpg, P]), ALU.mult))
                    out_.append((ed, md, t_m, m_free))
                made = []
                for ed, md, t_m, m_free in out_:
                    t_hi = on_act([t_m, m_free], lambda e, _, ed=ed, md=md: e.mul(
                        md.buffer[0][:], ed.buffer[:], M_SCALE))
                    made.append((md, on_dve([t_hi, m_free], lambda e, _, ed=ed, md=md: e.scalar_tensor_tensor(
                        out=md.buffer[1][:], in0=ed.buffer[:], scalar=M_SCALE, in1=md.buffer[0][:],
                        op0=ALU.mult, op1=ALU.subtract))))
                    ed.done(made[-1][1])
                return made, t_a

            def before_chunk(u):
                c, hf = units[u]
                b, h0, bo = c // (chunks // batches), hf * hph, banks[5]
                st = state[b][:, hf * half:(hf + 1) * half]
                free = bo.take()
                t_o = on_pe([free, state_ready[b][hf]], lambda e, _: e.matmul(
                    bo.buffer[:], ct[:, c * P:(c + 1) * P], st, start=True, stop=True))
                t_sd = on_pool([t_o, decays], lambda e, _: e.tensor_tensor(
                    by_head(st, hd), by_head(st, hd),
                    heads_over(sml["dec"][:, c, :], h0, hph, hd), ALU.mult))
                y_ = yac[u % 2]
                y_free = y_.take()
                t_1 = on_dve([t_o, decays, y_free], lambda e, _: e.tensor_tensor(
                    by_head(y_.buffer[:], hd), by_head(bo.buffer[:], hd),
                    heads_over(sml["ecs"][:, c, :], h0, hph, hd), ALU.mult))
                bo.done(t_1)
                return st, t_sd, y_, t_1

            def scan(u, mats, from_state):
                c, hf = units[u]
                b = c // (chunks // batches)
                st, t_sd, y_, t_1 = from_state
                x_, _, t_sk, t_xe, t_xp = xes[u]
                g_, t_gz = gates[u]
                by, bs = banks[4], banks[6]
                free = by.take()
                for h in range(hph):
                    md, t_m = mats[h // hpg]
                    for n, (a, v_) in enumerate(split_passes(md.buffer, xdp)):
                        t_y = on_pe([free, t_m, t_xp], lambda e, _, h=h, a=a, v_=v_, n=n: e.matmul(
                            by.buffer[:, h * hd:(h + 1) * hd], a[:, (h % hpg) * P:(h % hpg + 1) * P],
                            v_[:, h * hd:(h + 1) * hd], start=(n == 0), stop=(n == 2)),
                            mark=(h % hpg == hpg - 1 and n == 2))
                    if h % hpg == hpg - 1:
                        md.done(t_y)
                xdp_s.done(t_y)
                free = bs.take()
                t_s = on_pe([free, t_xe, t_bk], lambda e, _: e.matmul(
                    bs.buffer[:], btok[:, c * P:(c + 1) * P], xst.buffer[:], start=True, stop=True))
                xst.done(t_s)
                t_2 = on_pool([t_1, t_sk], lambda e, _: e.tensor_tensor(
                    y_.buffer[:], y_.buffer[:], x_.buffer[:], ALU.add))
                x_.done(t_2)
                t_3 = on_dve([t_2, t_y], lambda e, _: e.scalar_tensor_tensor(
                    out=y_.buffer[:], in0=by.buffer[:], scalar=1.0 / (M_SCALE * XDT_SCALE),
                    in1=y_.buffer[:], op0=ALU.mult, op1=ALU.add))
                by.done(t_3)
                t_sa = on_dve([t_sd, t_s], lambda e, _: e.tensor_tensor(st, bs.buffer[:], st, ALU.add))
                bs.done(t_sa)
                state_ready[b][hf] = [t_sa]
                t_4 = on_dve([t_3, t_gz], lambda e, _: e.tensor_tensor(
                    y_.buffer[:], y_.buffer[:], g_.buffer[:], ALU.mult))
                g_.done(t_4)
                return t_4, y_, (t_y, t_s)

            y_parts = {}

            def turn_y(u, t_4, y_):
                c, hf = units[u]
                bk = banks[7]
                free = bk.take()
                per = half // P
                for j in range(per):
                    t_t = on_pe([free, t_4], lambda e, _, j=j: e.transpose(
                        bk.buffer[:, j * P:(j + 1) * P], y_.buffer[:, j * P:(j + 1) * P], idn[:]),
                        mark=(j == per - 1))
                y_.done(t_t)
                ks = slice(hf * per, (hf + 1) * per)
                if hf == 0:
                    y_parts["free"], y_parts["ready"] = yt_s.take(), []
                src = bk.buffer[:].rearrange("p (k t) -> p k t", k=per)
                down = Y_SCALE / (2.0 * XN_SCALE * W_SCALE)
                t_hi = on_act([t_t, y_parts["free"]], lambda e, _: e.mul(yt[0][:, ks, :], src, down))
                t_lo = on_dve([t_hi, y_parts["free"]], lambda e, _: e.scalar_tensor_tensor(
                    out=yt[1][:, ks, :], in0=src, scalar=down, in1=yt[0][:, ks, :],
                    op0=ALU.mult, op1=ALU.subtract))
                bk.done(t_hi, t_lo)
                y_parts["ready"] += [t_hi, t_lo]

            attn = {}

            def project_out(c):
                bk = banks[7]
                free = bk.take()
                y_ready = y_parts["ready"]
                n = 0
                for k in range(ki):
                    for a, b in split_passes(yt, wo):
                        n += 1
                        t_p = on_pe([free, y_ready] if n == 1 else [], lambda e, _, k=k, a=a, b=b, n=n: e.matmul(
                            bk.buffer[:], a[:, k, :], b[:, k, :], start=(n == 1), stop=(n == 3 * ki)),
                            mark=(n == 3 * ki))
                yt_s.done(t_p)
                r = res[c]
                free = r.take()
                landed = load([free], lambda e, blk: e.dma_start(r.buffer[:], rows(x, c, blk)), st_res[c])
                t_r = on_dve([t_p, landed], lambda e, _: e.scalar_tensor_tensor(
                    out=r.buffer[:], in0=bk.buffer[:], scalar=1.0 / (Y_SCALE * W_SCALE), in1=r.buffer[:],
                    op0=ALU.mult, op1=ALU.add))
                bk.done(t_r)
                attn[c] = t_r

            state_ready = [[[state_made["loop"][b][hf]] if last else
                            [lambda b=b, hf=hf: [state_made["loop"][b][hf].before()]]
                            for hf in range(halves)] for b in range(batches)]
            project_x(0)
            mats, t_arg = decay(0)
            done_y = None
            for u in range(len(units)):
                here = mats
                old = before_chunk(u)
                if u:
                    turn_y(*done_y)
                if u + 1 < len(units):
                    mats, t_arg = decay(u + 1)
                t_4, y_, t_scan = scan(u, here, old)
                done_y = (u, t_4, y_)
                if u + 1 < len(units):
                    project_x(u + 1)
                if u and units[u - 1][1] == halves - 1:
                    project_out(units[u - 1][0])
                if u + 2 < len(units):
                    project_z(u + 2)
            small_s.done(t_4, t_scan[0], t_arg)
            gt_s.done(t_4)
            state_made[pr.section] = [[state_ready[b][hf][0] for hf in range(halves)]
                                      for b in range(batches)]
            arena_s.done(xes[len(units) - 1][1])
            arena_b.done(*t_scan)

            s_free, b_free = arena_s.take(), arena_b.take()
            h_ready, mids = [], {}

            def ffn_up(m):
                ts = []
                for j in range(2):
                    bk = banks[2 * (m % 2) + j]
                    free = bk.take()
                    n = 0
                    for k in range(kd):
                        for part in xt:
                            n += 1
                            t = on_pe([free], lambda e, _, j=j, k=k, part=part, bk=bk, n=n: e.matmul(
                                bk.buffer[:], q12[:, j, k, m * P:(m + 1) * P], part[:, k, :],
                                start=(n == 1), stop=(n == 2 * kd)), mark=(n == 2 * kd), apart=True)
                    ts.append((t, bk))
                (t_1, b1), (t_2, b2) = ts
                th, fl = tnh[m % 2], full[m % 2]
                th_free, fl_free = th.take(), fl.take()
                t_th = on_act([t_1, th_free], lambda e, _: e.activation(
                    th.buffer[:], b1.buffer[:], ACT.Tanh, scale=0.5 / XN_SCALE))
                b1.done(t_th)
                t_f = on_dve([t_th, t_2, fl_free], lambda e, _: e.scalar_tensor_tensor(
                    out=fl.buffer[:], in0=th.buffer[:], scalar=1.0, in1=b2.buffer[:],
                    op0=ALU.add, op1=ALU.mult))
                b2.done(t_f)
                th.done(t_f)
                mids[m] = (fl, t_f)
                return t_2

            def ffn_parts(m):
                fl, t_f = mids[m]
                hid_free = [s_free, b_free if (m + 1) * 2 * tb > after_s else []]
                hid_free = hid_free[0] + hid_free[1]
                t_hi = on_act([t_f, hid_free], lambda e, _: e.copy(hid[:, m, 0, :], fl.buffer[:]))
                t_lo = on_dve([t_hi, hid_free], lambda e, _: e.tensor_tensor(
                    hid[:, m, 1, :], fl.buffer[:], hid[:, m, 0, :], ALU.subtract))
                fl.done(t_lo)
                h_ready.append(t_lo)

            between, x_tok = ([], []) if last else norm(1)
            for m in range(kf):
                t_2 = ffn_up(m)
                if m == 0:
                    turn_y(*done_y)
                if m == 1:
                    project_out(units[-1][0])
                if m:
                    ffn_parts(m - 1)
                if m >= 2 and between:
                    between.pop(0)()
            while between:
                between.pop(0)()
            if not last:
                xt_made["loop"] = turn(x_tok, t_2)
            ffn_parts(kf - 1)

            for c in range(chunks):
                bk = banks[c]
                free = bk.take()
                n = 0
                for m in range(kf):
                    for p in range(2):
                        n += 1
                        t_p = on_pe([free, h_ready[m]], lambda e, _, m=m, p=p, c=c, bk=bk, n=n: e.matmul(
                            bk.buffer[:], hid[:, m, p, c * P:(c + 1) * P], q3[:, m, :],
                            start=(n == 1), stop=(n == 2 * kf)), mark=(n == 2 * kf), apart=True)
                r = res[c]
                t_r = on_dve([t_p, attn[c]], lambda e, _, r=r, bk=bk: e.scalar_tensor_tensor(
                    out=r.buffer[:], in0=bk.buffer[:], scalar=1.0 / HID_SCALE, in1=r.buffer[:],
                    op0=ALU.mult, op1=ALU.add))
                bk.done(t_r)
                stored = load([t_r], lambda e, blk, r=r, c=c: e.dma_start(rows(out, c, blk), r.buffer[:]), st_out[c])
                r.done(stored)
            arena_s.done(t_p)
            arena_b.done(t_p)

        xt_made, state_made = {}, {}
        engines = ("tensor", "scalar", "vector", "gpsimd", "sync")
        for name in engines:
            pr.step(name, set_up, lambda e, _: None)
        t_z = on_dve([], lambda e, _: e.memset(ap3[:], 0.0))
        steps, x_tok = norm(0)
        for step in steps:
            step()
        xt_first = turn(x_tok, [])
        pr.section = "loop"
        body(False)
        pr.section = "last"
        body(True)
        finals = [t for s in st_out for t in [Token(s, "last", s.counts["last"])]]
        pr.step("sync", finals, lambda e, _: None)

        credit = {"tensor": [pe], "scalar": [act], "vector": [dve], "gpsimd": [pool],
                  "sync": [*st_x, *st_res, *st_out, st_rows]}
        block = ctx.enter_context(nc.Block())

        def emit(name):
            def run(eng):
                for s in credit[name]:
                    if s.counts["loop"]:
                        eng.sem_inc(s.sem["block"], s.counts["loop"])
                pr.play(name, eng, "setup", 0)
                with eng.Fori(0, nb - 1) as i:
                    pr.play(name, eng, "loop", i)
                pr.play(name, eng, "last", nb - 1)
            return run

        block.tensor(emit("tensor"))
        block.scalar(emit("scalar"))
        block.vector(emit("vector"))
        block.gpsimd(emit("gpsimd"))
        block.sync(emit("sync"))


def kernel(**inputs):
    import concourse.bacc as bacc
    from concourse.bass_utils import run_bass_kernel_spmd

    def get(name):
        return np.asarray(inputs[name])

    def tiles(w):
        n, k = w.shape
        return np.ascontiguousarray(w.T.reshape(k // P, P, n).transpose(1, 0, 2).reshape(P, -1))

    heads, chunks = 16, 4
    w_x = get("L0_attn_x_proj_w")
    di = w_x.shape[1]
    cw = get("L0_attn_conv_w")
    ki = cw.shape[0] // P
    bf16 = np.dtype("bfloat16")
    s_, l_ = np.arange(P)[:, None], np.arange(P)[None, :]
    mask_neg = np.tile(np.where(l_ < s_, -1e30, 0.0), (1, 4)).astype(bf16)
    upper = (s_ <= l_).astype(np.float32)
    cs_lhs = np.zeros((P, chunks, P), bf16)
    cs_rhs = np.zeros((P, heads, P), bf16)
    for c in range(chunks):
        cs_lhs[96 + 3 * c:99 + 3 * c, c, :] = 1
    for j in range(3):
        for h in range(heads):
            cs_rhs[32 * j + h, h, :] = 1
    arrays = {
        "x": get("L0_attn_x"),
        "w_in": np.ascontiguousarray(get("L0_attn_in_proj_w").T),
        "conv_w": np.ascontiguousarray(cw.reshape(ki, P, -1).transpose(1, 0, 2)),
        "conv_b": np.ascontiguousarray(get("L0_attn_conv_b").reshape(ki, P).T),
        "w_x": np.ascontiguousarray(np.concatenate([w_x[:di], w_x[di + heads:]]).T),
        "w_xdt": np.ascontiguousarray(w_x[di:di + heads]),
        "w_dt": np.ascontiguousarray(get("L0_attn_dt_proj_w").T),
        "dt_bias": get("L0_attn_dt_proj_b"),
        "a_log": get("L0_attn_A_log"),
        "d_skip": get("L0_attn_D"),
        "w_out": np.ascontiguousarray(get("L0_attn_out_proj_w").T),
        "w_ffn": np.concatenate([tiles(get(f"L0_ffn_w{n}")) for n in (1, 2, 3)], axis=1),
        "ident": np.eye(P, dtype=np.float32),
        "mask_neg": mask_neg,
        "upper": upper,
        "cs_lhs": cs_lhs,
        "cs_rhs": cs_rhs.reshape(P, heads * P),
    }
    nc = bacc.Bacc("TRN2", target_bir_lowering=False, num_devices=1, dynamic_dma_scratch_size=1024)
    args = [nc.dram_tensor(n, a.shape, mybir.dt.from_np(a.dtype), kind="ExternalInput").ap()
            for n, a in arrays.items()]
    out = nc.dram_tensor("out", arrays["x"].shape, F32, kind="ExternalOutput").ap()
    mamba_ffn_block(nc, *args, out)
    return run_bass_kernel_spmd(nc, [arrays], core_ids=[0]).results[0]["out"]
```

```python
from contextlib import ExitStack

import numpy as np

import concourse.bass as bass
from concourse import mybir

ACT = mybir.ActivationFunctionType
ALU = mybir.AluOpType
F32 = mybir.dt.float32
F16 = mybir.dt.float16
BF16 = mybir.dt.bfloat16
FP8 = mybir.dt.float8e4

P = 128
DMA = 16

XN_SCALE = 2.0 ** 5
W_SCALE = 2.0 ** 8
CONV_SCALE = 2.0 ** 7
S_SCALE = 2.0 * CONV_SCALE
Y_SCALE = 2.0 ** 10
XDT_SCALE = 2.0 ** 10
M_SCALE = 2.0 ** 6
HID_SCALE = 2.0 * XN_SCALE


class Token:

    def __init__(self, stream, section, count, earlier=0):
        self.stream, self.section, self.count, self.earlier = stream, section, count, earlier

    def before(self):
        return Token(self.stream, self.section, self.count, self.earlier + 1)


class Stream:

    def __init__(self, name, setup_sem, block_sem, step=1):
        self.name, self.sem, self.step = name, {"setup": setup_sem, "block": block_sem}, step
        self.counts = {"setup": 0, "loop": 0, "last": 0}

    def mark(self, section):
        self.counts[section] += self.step
        return Token(self, section, self.counts[section])


class Program:

    def __init__(self):
        self.queues = {}
        self.section = "setup"

    def step(self, engine, waits, issue, stream=None, apart=False):
        token = stream.mark(self.section) if stream else None
        flat = []
        for w in waits:
            flat += w if isinstance(w, (list, tuple)) else [w]
        self.queues.setdefault((engine, self.section), []).append(
            (flat, issue, stream, apart))
        return token

    def play(self, engine, handle, section, block):
        reached = {}
        for waits, issue, stream, apart in self.queues.get((engine, section), []):
            waited = False
            for t in waits:
                if t is None:
                    continue
                if callable(t):
                    t = t()
                    if t is None:
                        continue
                    ts = t if isinstance(t, list) else [t]
                else:
                    ts = [t]
                for t in ts:
                    per = t.stream.counts["loop"]
                    if t.section == "setup":
                        sem, level = t.stream.sem["setup"], t.count
                        key = (t.stream.name, "setup")
                        if reached.get(key, 0) >= level:
                            continue
                        reached[key] = level
                        handle.wait_ge(sem, level)
                        continue
                    sem, key = t.stream.sem["block"], (t.stream.name, "block")
                    back = t.earlier if t.section == section else 1
                    level = t.count - back * per
                    if reached.get(key, -10 ** 9) >= level:
                        continue
                    reached[key] = level
                    handle.wait_ge(sem, block * per + (per + level))
                    waited = True
            if apart and waited:
                handle.sem_inc(self.passed, 1)
            made = issue(handle, block)
            if stream is not None:
                made.then_inc(stream.sem["setup" if section == "setup" else "block"], stream.step)


class Slot:

    def __init__(self, program, buffer=None):
        self.program, self.buffer = program, buffer
        self.uses = {"setup": [], "loop": [], "last": []}

    def take(self):
        section = self.program.section
        uses = self.uses[section]
        uses.append([])
        n = len(uses) - 1
        if n:
            assert uses[n - 1], "taken before its last user's readers are known"
            return list(uses[n - 1])
        if section == "setup":
            return []
        last = self.uses["loop"]
        if section == "last":
            return list(last[-1])
        start = self.uses["setup"][-1] if self.uses["setup"] else []
        return [*start, lambda: [t.before() for t in last[-1]]]

    def done(self, *tokens):
        self.uses[self.program.section][-1] += tokens


def mamba_ffn_block(nc, x, w_in, conv_w, conv_b, w_x, w_xdt, w_dt, dt_bias, a_log, d_skip, w_out,
                    w_ffn, ident, mask_neg, upper, cs_rows, cs_heads, out):
    batches, seqlen, dm = x.shape
    di = w_in.shape[1] // 2
    heads = w_dt.shape[0]
    hd = di // heads
    ns = (w_x.shape[1] - di) // 2
    fh = (w_ffn.shape[1]) // (3 * dm) * P
    tb = 512
    nb = batches * seqlen // tb
    span = tb // batches
    chunks = tb // P
    kd, ki, kf = dm // P, di // P, fh // P
    taps = conv_w.shape[2]
    halo = taps - 1
    half = 512
    halves = di // half
    hph = half // hd
    hpg = half // P
    assert batches == 2 and ns == P and chunks == 4 and dm == half and heads == 16

    pr = Program()
    ctx = ExitStack()
    with ctx:
        def sem(name):
            return ctx.enter_context(nc.semaphore(name))

        pr.passed = sem("passed")

        def stream(name, step=1):
            return Stream(name, sem(name + "_setup"), sem(name + "_blocks"), step)

        def sb(name, shape, dt=F32, where=ctx):
            return where.enter_context(nc.sbuf_tensor(name, shape, dt))

        pe, act, dve, pool = (stream(n) for n in ("pe", "act", "dve", "pool"))
        st_x = [stream(f"x_in{n}", DMA) for n in range(4)]
        st_res = [stream(f"residual{c}", DMA) for c in range(chunks)]
        st_out = [stream(f"stored{c}", DMA) for c in range(chunks)]
        st_small = stream("small", DMA)
        streams = [pe, act, dve, pool, *st_x, *st_res, *st_out]

        def on_pe(waits, issue, mark=True, apart=False):
            return pr.step("tensor", waits, issue, pe if mark else None, apart)

        def on_act(waits, issue):
            return pr.step("scalar", waits, issue, act)

        def on_dve(waits, issue, apart=False):
            return pr.step("vector", waits, issue, dve, apart)

        def on_pool(waits, issue, apart=False):
            return pr.step("gpsimd", waits, issue, pool, apart)

        def load(waits, issue, st):
            return pr.step("sync", waits, issue, st)

        win = [sb(f"win_{p}", [P, kd, 2 * di], F16) for p in ("hi", "lo")]
        wx = [sb(f"wx_{p}", [P, ki, w_x.shape[1]], F16) for p in ("hi", "lo")]
        wo = [sb(f"wo_{p}", [P, ki, dm], F16) for p in ("hi", "lo")]
        q12 = sb("q12", [P, 2, kd, fh], FP8)
        q3 = sb("q3", [P, kf, dm], FP8)
        idn = sb("idn", [P, P])
        idb = sb("idb", [P, P], BF16)
        neg = sb("neg", [P, half], BF16)
        upp = sb("upp", [P, P])
        ones = sb("ones", [P, P])
        csr = sb("csr", list(cs_rows.shape))
        csh = sb("csh", list(cs_heads.shape), BF16)
        cw = sb("cw", [P, ki, taps])
        cws = sb("cws", [P, ki])
        cb = sb("cb", [P, ki])
        w2 = [sb(f"w2_{p}", [P, ki, heads], F16) for p in ("hi", "lo")]
        dtb = sb("dtb", [P, heads])
        na = sb("na", [P, heads])
        dsk = sb("dsk", [P, heads])
        mhalf = sb("mhalf", [P, chunks])
        thr = sb("thr", [P, 3])
        nthr = sb("nthr", [P, 3])
        state = [sb(f"state{b}", [P, di]) for b in range(batches)]
        hal = sb("hal", [P, ki, batches, halo])

        banks = [Slot(pr, ctx.enter_context(nc.psum_tensor(f"bank{n}", [P, half], F32)))
                 for n in range(8)]

        early = ExitStack()
        stg_n = 2
        stage = [Slot(pr, sb(f"stage{n}", [P, 2 * di], where=early)) for n in range(stg_n)]
        st_stage = [stream(f"stage{n}", DMA) for n in range(stg_n)]
        ffn = [sb(f"ffn{n}", [P, kd * fh], where=early) for n in range(3)]
        st_ffn = [stream(f"ffn{n}", DMA) for n in range(3)]
        junk = Slot(pr, sb("junk", [P, fh], BF16, where=early))
        below = [Slot(pr, sb(f"below{n}", [P, fh], BF16, where=early)) for n in range(2)]
        asum = sb("asum", [P, 3, kd], where=early)
        tsum = sb("tsum", [P, 3], where=early)
        gam = sb("gam", [P, 3], where=early)

        wdt = sb("wdt", [heads, heads], where=early)
        wxdt = sb("wxdt", [heads, di], where=early)
        small = None
        for dst, src in ((idn, ident), (neg, mask_neg), (upp, upper), (csr, cs_rows),
                         (csh, cs_heads), (cw, conv_w), (cb, conv_b), (wdt, w_dt),
                         (wxdt, w_xdt)):
            small = load([], lambda e, _, dst=dst, src=src: e.dma_start(dst[:], src), st_small)
        for dst, src in ((dtb, dt_bias), (na, a_log), (dsk, d_skip)):
            small = load([], lambda e, _, dst=dst, src=src: e.dma_start(
                dst[:], src.unsqueeze(0).to_broadcast([P, heads])), st_small)

        pieces = []
        for k in range(kd):
            pieces.append((w_in[k * P:(k + 1) * P, :], 2 * di, [w[:, k, :] for w in win]))
        for k in range(ki):
            pieces.append((w_x[k * P:(k + 1) * P, :], w_x.shape[1], [w[:, k, :] for w in wx]))
        for k in range(ki):
            pieces.append((w_out[k * P:(k + 1) * P, :], dm, [w[:, k, :] for w in wo]))
        for n, (src, cols, (hi, lo)) in enumerate(pieces):
            s = stage[n % stg_n]
            buf = s.buffer
            free = s.take()
            landed = load(free, lambda e, _, buf=buf, cols=cols, src=src: e.dma_start(
                buf[:, 0:cols], src), st_stage[n % stg_n])
            t_hi = on_act([landed], lambda e, _, hi=hi, buf=buf, cols=cols: e.activation(
                hi, buf[:, 0:cols], ACT.Copy, scale=W_SCALE))
            t_lo = on_dve([landed, t_hi], lambda e, _, hi=hi, lo=lo, buf=buf, cols=cols:
                          e.scalar_tensor_tensor(out=lo, in0=buf[:, 0:cols], scalar=W_SCALE,
                                                 in1=hi, op0=ALU.mult, op1=ALU.subtract))
            s.done(t_hi, t_lo)
            if n < 3:
                j = n
                st = load([], lambda e, _, j=j: e.dma_start(
                    ffn[j][:], w_ffn[:, j * kd * fh:(j + 1) * kd * fh]), st_ffn[j])
                ffn_in = [st] if n == 0 else ffn_in + [st]

        t_one = on_pool([], lambda e, _: e.memset(ones[:], 1.0))
        t_clear = [on_pool([], lambda e, _, b=b: e.memset(state[b][:], 0.0)) for b in range(batches)]
        t_clear.append(on_pool([], lambda e, _: e.memset(hal[:], 0.0)))
        t_clear.append(on_pool([], lambda e, _: e.memset(mhalf[:], -0.5)))

        free = banks[1].take()
        for k in range(ki):
            t_w2 = on_pe([small, free], lambda e, _, k=k: e.matmul(
                banks[1].buffer[:, k * heads:(k + 1) * heads], wxdt[:, k * P:(k + 1) * P], wdt[:],
                start=True, stop=True))
        flat = [w[:].rearrange("p k h -> p (k h)") for w in w2]
        t_hi = on_act([t_w2], lambda e, _: e.activation(
            flat[0], banks[1].buffer[:, 0:ki * heads], ACT.Copy, scale=W_SCALE))
        t_w2 = on_dve([t_hi], lambda e, _: e.scalar_tensor_tensor(
            out=flat[1], in0=banks[1].buffer[:, 0:ki * heads], scalar=W_SCALE, in1=flat[0],
            op0=ALU.mult, op1=ALU.subtract))
        banks[1].done(t_hi, t_w2)

        for j in range(3):
            for k in range(kd):
                free = junk.take()
                t_abs = on_act([ffn_in[j], free], lambda e, _, j=j, k=k: e.activation(
                    junk.buffer[:], ffn[j][:, k * fh:(k + 1) * fh], ACT.Abs,
                    accum_out=asum[:, j, k:k + 1]))
                junk.done(t_abs)
        t_sum = on_dve([t_abs], lambda e, _: e.reduce_sum(tsum[:], asum[:], mybir.AxisListType.X))
        free = banks[0].take()
        t_tot = on_pe([t_sum, t_one], lambda e, _: e.matmul(
            banks[0].buffer[:, 0:3], ones[:], tsum[:], start=True, stop=True))
        t_gam = on_dve([t_tot], lambda e, _: e.tensor_scalar(
            gam[:], banks[0].buffer[:, 0:3], 1.0 / (dm * fh), 1e-8, ALU.mult, ALU.add))
        banks[0].done(t_gam)
        t_thr = on_dve([t_gam], lambda e, _: e.tensor_scalar(thr[:], gam[:], 0.5, None, ALU.mult))
        t_thr = on_dve([t_gam], lambda e, _: e.tensor_scalar(nthr[:], gam[:], -0.5, None, ALU.mult))
        for j in range(3):
            for k in range(kd):
                w = ffn[j][:, k * fh:(k + 1) * fh]
                q = q12[:, j, k, :] if j < 2 else q3[:].rearrange("p k n -> p (k n)")[:, k * fh:(k + 1) * fh]
                bl = below[k % 2]
                free = bl.take()
                t_b = on_dve([t_thr, free], lambda e, _, w=w, j=j, bl=bl: e.tensor_scalar(
                    bl.buffer[:], w, nthr[:, j:j + 1], None, ALU.is_lt))
                t_q = on_dve([t_b], lambda e, _, w=w, j=j, q=q, bl=bl: e.scalar_tensor_tensor(
                    out=q, in0=w, scalar=thr[:, j:j + 1], in1=bl.buffer[:], op0=ALU.is_gt,
                    op1=ALU.subtract, saturate=False))
                bl.done(t_q)
        t_exp = on_act([small], lambda e, _: e.activation(na[:], na[:], ACT.Exp))
        on_dve([t_exp], lambda e, _: e.tensor_scalar(na[:], na[:], -1.0, None, ALU.mult))
        on_dve([small], lambda e, _: e.tensor_copy(idb[:], idn[:]))
        t_cws = on_dve([small], lambda e, _: e.tensor_scalar(
            cws[:], cw[:, :, taps - 1], CONV_SCALE / (XN_SCALE * W_SCALE), None, ALU.mult))
        t_cw = on_dve([small, t_cws], lambda e, _: e.tensor_scalar(cw[:], cw[:], CONV_SCALE, None, ALU.mult))
        t_cb = on_dve([small], lambda e, _: e.tensor_scalar(cb[:], cb[:], CONV_SCALE, None, ALU.mult))
        set_up = [t_q, t_cb, t_lo, t_exp, t_clear[-1]]
        early.close()

        stats = sb("stats", [P, chunks, 6])
        mv = sb("mv", [P, chunks, 2])
        rstd = sb("rstd", [P, chunks])
        rstd_s = Slot(pr)
        xt = [sb(f"xt_{p}", [P, kd, tb], F16) for p in ("hi", "lo")]
        raw = [Slot(pr, sb(f"raw{n}", [P, batches, halo + span])) for n in range(2)]
        tnh = [Slot(pr, sb(f"tnh{n}", [P, tb])) for n in range(2)]
        full = [Slot(pr, sb(f"full{n}", [P, tb])) for n in range(2)]
        arena = sb("arena", [P, 2 * kf * tb], F16)
        s_parts = [arena[:, p * ki * tb:(p + 1) * ki * tb].rearrange("p (k t) -> p k t", k=ki)
                   for p in range(2)]
        after_s = 2 * ki * tb
        bt = arena[:, after_s:after_s + 2 * tb].bitcast(F32)
        ct = arena[:, after_s + 2 * tb:after_s + 4 * tb].bitcast(F32)
        btok = arena[:, after_s + 4 * tb:after_s + 6 * tb].bitcast(F32)
        hid = arena[:].rearrange("p (k q t) -> p k q t", k=kf, q=2)
        arena_s, arena_b = Slot(pr), Slot(pr)
        gt = sb("gt", [P, chunks, P])
        gt_s = Slot(pr)
        sml = {n: sb(n, [P, chunks, heads]) for n in
               ("dtv", "dab", "du", "dz", "dq", "dp", "dt", "av", "cs", "ecs", "dst", "dec")}
        cs_k = 6 * heads
        ap6 = sb("ap6", [P, chunks, 6, heads])
        lhs_cs = sb("lhs_cs", [cs_k, tb], BF16)
        csq = sb("csq", [cs_k, tb], BF16)
        rhs_cs = [Slot(pr, sb(f"rhs_cs{n}", [cs_k, hph * P], BF16)) for n in range(2)]
        small_s = Slot(pr)
        xs = [Slot(pr, sb(f"xs{n}", [P, half])) for n in range(2)]
        xdt = Slot(pr, sb("xdt", [P, half]))
        xdp = [sb(f"xdt_{p}", [P, half], F16) for p in ("hi", "lo")]
        xdp_s = Slot(pr)
        xst = Slot(pr, sb("xst", [P, half]))
        yac = [Slot(pr, sb(f"yac{n}", [P, half])) for n in range(2)]
        gate = [Slot(pr, sb(f"gate{n}", [P, half])) for n in range(2)]
        xin = [*yac, *gate]
        edc = [Slot(pr, sb(f"edc{n}", [P, hpg * P])) for n in range(2)]
        mdc = [Slot(pr, sb(f"mdc{n}", [P, 2, hpg * P], F16)) for n in range(4)]
        branch = [(sl, sl.buffer[:]) for sl in (*edc, *xs)]
        branch += [(sl, sl.buffer[:].rearrange("p q t -> p (q t)").bitcast(F32)) for sl in mdc]
        yt = [sb(f"yt_{p}", [P, ki, P], F16) for p in ("hi", "lo")]
        yt_s = Slot(pr)
        res = [Slot(pr, sb(f"res{c}", [P, dm])) for c in range(chunks)]

        def heads_over(v, h0, n, width):
            return v[:, h0:h0 + n].unsqueeze(2).to_broadcast([P, n, width])

        def by_head(v, width):
            return v.rearrange("p (h d) -> p h d", d=width)

        def rows(dram, c, block):
            b, at = c // (chunks // batches), (c % (chunks // batches)) * P
            if isinstance(block, int):
                return dram[b, block * span + at:block * span + at + P, :]
            return dram[b, bass.ds(block * span + at, P), :]

        def split_passes(a, b):
            return [(a[0], b[0]), (a[0], b[1]), (a[1], b[0])]

        def norm(shift):
            x_tok, seen = [], {}

            def statistics(c):
                if c == 0:
                    seen["free"] = rstd_s.take()
                s = xin[c]
                free = s.take()
                landed = load([free], lambda e, blk: e.dma_start(
                    s.buffer[:], rows(x, c, blk + shift)), st_x[c])
                t = on_dve([landed, seen["free"]], lambda e, _: e.bn_stats(stats[:, c, :], s.buffer[:]))
                seen["mv", c] = on_dve([t], lambda e, _: e.bn_aggr(mv[:, c, :], stats[:, c, :]), apart=True)

            def root():
                t = on_dve([seen["mv", chunks - 1]], lambda e, _: e.tensor_scalar(
                    rstd[:], mv[:, :, 1], 1e-5, None, ALU.add))
                t = on_pool([t], lambda e, _: e.tensor_tensor(rstd[:], rstd[:], mhalf[:], ALU.pow))
                seen["root"] = on_dve([t], lambda e, _: e.tensor_scalar(
                    rstd[:], rstd[:], XN_SCALE, None, ALU.mult))

            def normalise(c):
                s = xin[c]
                t = on_dve([seen["root"]], lambda e, _: e.tensor_scalar(
                    s.buffer[:], s.buffer[:], mv[:, c, 0:1], rstd[:, c:c + 1], ALU.subtract, ALU.mult))
                x_tok.append(t)
                if c == chunks - 1:
                    rstd_s.done(t)

            steps = [lambda c=c: statistics(c) for c in range(chunks)]
            steps += [root] + [lambda c=c: normalise(c) for c in range(chunks)]
            return steps, x_tok

        def turn(x_tok, xt_free):
            for k in range(kd):
                bk = banks[4 + k]
                free = bk.take()
                for c in range(chunks):
                    t_t = on_pe([free, x_tok[c]], lambda e, _, k=k, c=c, bk=bk: e.transpose(
                        bk.buffer[:, c * P:(c + 1) * P], xin[c].buffer[:, k * P:(k + 1) * P], idn[:]),
                        mark=(c == chunks - 1))
                t_hi = on_act([t_t, xt_free], lambda e, _, k=k, bk=bk: e.copy(xt[0][:, k, :], bk.buffer[:]))
                t_lo = on_dve([t_hi, xt_free], lambda e, _, k=k, bk=bk: e.tensor_tensor(
                    xt[1][:, k, :], bk.buffer[:], xt[0][:, k, :], ALU.subtract))
                bk.done(t_hi, t_lo)
            for s in xin:
                s.done(t_t)
            return t_lo

        def x_branch(m, xt_ready, cleared=()):
            bk = banks[4 + m % 4]
            free = bk.take()
            n = 0
            for k in range(kd):
                for a, b in split_passes(win, xt):
                    n += 1
                    t_mm = on_pe([free, xt_ready] if n == 1 else [],
                                 lambda e, _, k=k, a=a, b=b, n=n: e.matmul(
                                     bk.buffer[:], a[:, k, m * P:(m + 1) * P], b[:, k, :],
                                     start=(n == 1), stop=(n == 3 * kd)),
                                 mark=(n == 3 * kd))
            r, (a_, ab), tp = raw[m % 2], branch[m], (xdt, xst)[m % 2]
            r_free, a_free, p_free = r.take(), a_.take(), tp.take()
            acc3 = ab.rearrange("p (b t) -> p b t", b=batches)
            tp3 = tp.buffer[:].rearrange("p (b t) -> p b t", b=batches)
            t_h = on_pool([r_free, cleared], lambda e, _: e.tensor_copy(
                r.buffer[:, :, 0:halo], hal[:, m, :, :]), apart=True)
            t_raw = on_act([t_mm, r_free], lambda e, _: e.activation(
                r.buffer[:, :, halo:], bk.buffer[:].rearrange("p (b t) -> p b t", b=batches),
                ACT.Copy, scale=1.0 / (XN_SCALE * W_SCALE)))
            t_acc = on_act([a_free], lambda e, _: e.activation(
                ab, bk.buffer[:], ACT.Identity, scale=cws[:, m:m + 1], bias=cb[:, m:m + 1]))
            bk.done(t_acc)
            t_h2 = on_pool([t_h, t_raw], lambda e, _: e.tensor_copy(
                hal[:, m, :, :], r.buffer[:, :, span:span + halo]), apart=True)
            t_tap = on_act([t_h, t_raw, p_free], lambda e, _: e.mul(
                tp3, r.buffer[:, :, halo - 1:halo - 1 + span], cw[:, m, halo - 1:halo]))
            t_c = on_pool([t_acc, t_tap], lambda e, _: e.tensor_tensor(
                ab, ab, tp.buffer[:], ALU.add))
            tp.done(t_c)
            for j in range(halo - 1):
                t_c = on_dve([t_c, t_h2], lambda e, _, j=j: e.scalar_tensor_tensor(
                    out=acc3, in0=r.buffer[:, :, j:j + span],
                    scalar=cw[:, m, j:j + 1], in1=acc3, op0=ALU.mult, op1=ALU.add))
            r.done(t_c, t_h2, t_tap)
            return a_, ab, t_c

        def silu(m, a_, ab, t_c):
            th = tnh[m % 2]
            th_free = th.take()
            t_th = on_act([t_c, th_free], lambda e, _: e.activation(
                th.buffer[:], ab, ACT.Tanh, scale=0.5 / CONV_SCALE))
            t_f = on_dve([t_th], lambda e, _: e.scalar_tensor_tensor(
                out=ab, in0=th.buffer[:], scalar=1.0, in1=ab, op0=ALU.add, op1=ALU.mult))
            th.done(t_f)
            a_.done(t_f)
            return t_f

        def body(last):
            def from_before(made, first):
                return [made["loop"]] if last else [first, lambda: [made["loop"].before()]]

            xt_ready = from_before(xt_made, xt_first)
            s_free, b_free = arena_s.take(), arena_b.take()
            s_ready = []

            def branch_parts(m):
                a_, ab = branch[m]
                a_.take()
                t_f = from_before(branch_made[m], branch_first[m])
                t_hi = on_act([t_f, s_free], lambda e, _: e.copy(s_parts[0][:, m, :], ab))
                t_lo = on_dve([t_f, t_hi, s_free], lambda e, _: e.tensor_tensor(
                    s_parts[1][:, m, :], ab, s_parts[0][:, m, :], ALU.subtract))
                a_.done(t_hi, t_lo)
                s_ready.append(t_lo)

            for m in range(ki):
                branch_parts(m)

            order = [0, 2, 1, 3]
            units = [(c, hf) for c in order for hf in range(halves)]
            gates, xes = {}, {}

            def project_z(u):
                c, hf = units[u]
                bz = banks[1]
                free = bz.take()
                n = 0
                for k in range(kd):
                    for a, b in split_passes(xt, win):
                        n += 1
                        t_z = on_pe([free, xt_ready], lambda e, _, k=k, a=a, b=b, n=n: e.matmul(
                            bz.buffer[:], a[:, k, c * P:(c + 1) * P],
                            b[:, k, di + hf * half:di + (hf + 1) * half],
                            start=(n == 1), stop=(n == 3 * kd)), mark=(n == 3 * kd))
                g_, th = gate[u % 2], tnh[u % 2]
                g_free, th_free = g_.take(), th.take()
                t_th = on_act([t_z, th_free], lambda e, _: e.activation(
                    th.buffer[:], bz.buffer[:], ACT.Tanh, scale=0.5 / (XN_SCALE * W_SCALE)))
                t_gz = on_dve([t_th, g_free], lambda e, _: e.scalar_tensor_tensor(
                    out=g_.buffer[:], in0=th.buffer[:], scalar=1.0, in1=bz.buffer[:],
                    op0=ALU.add, op1=ALU.mult))
                bz.done(t_gz)
                th.done(t_gz)
                gates[u] = (g_, t_gz)

            project_z(0)

            def project(bk, col, width):
                free = bk.take()
                n = 0
                for k in range(ki):
                    for a, b in split_passes(wx, s_parts):
                        n += 1
                        t = on_pe([free, s_ready[k]], lambda e, _, k=k, a=a, b=b, n=n: e.matmul(
                            bk.buffer[0:width, :], a[:, k, col:col + width], b[:, k, :],
                            start=(n == 1), stop=(n == 3 * ki)), mark=(n == 3 * ki))
                return t

            unscale = 1.0 / (S_SCALE * W_SCALE)
            t_b = project(banks[3], di, ns)
            t_bt = on_act([t_b, b_free], lambda e, _: e.mul(bt, banks[3].buffer[:], unscale))
            banks[3].done(t_bt)
            sm_free = small_s.take()
            free = banks[2].take()
            for c in range(chunks):
                n = 0
                for k in range(ki):
                    for a, b in split_passes(s_parts, w2):
                        n += 1
                        t_dp = on_pe([free, s_ready[k]], lambda e, _, c=c, k=k, a=a, b=b, n=n: e.matmul(
                            banks[2].buffer[:, c * heads:(c + 1) * heads], a[:, k, c * P:(c + 1) * P],
                            b[:, k, :], start=(n == 1), stop=(n == 3 * ki)),
                            mark=(c == chunks - 1 and n == 3 * ki))
            v = {n: t[:].rearrange("p c h -> p (c h)") for n, t in sml.items()}
            t1 = on_dve([t_dp, sm_free], lambda e, _: e.scalar_tensor_tensor(
                out=sml["dtv"][:], scalar=unscale, op0=ALU.mult, op1=ALU.add,
                in0=banks[2].buffer[:, 0:chunks * heads].rearrange("p (c h) -> p c h", h=heads),
                in1=dtb[:].unsqueeze(1).to_broadcast([P, chunks, heads])))
            banks[2].done(t1)
            t2 = on_dve([t1], lambda e, _: e.scalar_tensor_tensor(
                out=v["dab"], in0=v["dtv"], scalar=-1.0, in1=v["dtv"], op0=ALU.mult, op1=ALU.max))
            t3 = on_act([t2], lambda e, _: e.activation(v["du"], v["dab"], ACT.Exp, scale=-1.0))
            t4 = on_dve([t3], lambda e, _: e.tensor_scalar(v["dab"], v["du"], 2.0, None, ALU.add))
            t4 = on_dve([t4], lambda e, _: e.reciprocal(v["dz"], v["dab"]))
            t4 = on_dve([t4], lambda e, _: e.tensor_tensor(v["dz"], v["dz"], v["du"], ALU.mult))
            t4 = on_dve([t4], lambda e, _: e.tensor_tensor(v["dq"], v["dz"], v["dz"], ALU.mult))
            t4 = on_dve([t4], lambda e, _: e.tensor_scalar(v["dp"], v["dq"], 1.0 / 17, None, ALU.mult))
            for odd in range(15, 1, -2):
                t4 = on_dve([t4], lambda e, _, odd=odd: e.scalar_tensor_tensor(
                    out=v["dp"], in0=v["dp"], scalar=1.0 / odd, in1=v["dq"], op0=ALU.add, op1=ALU.mult))
            t4 = on_dve([t4], lambda e, _: e.scalar_tensor_tensor(
                out=v["dp"], in0=v["dp"], scalar=1.0, in1=v["dz"], op0=ALU.add, op1=ALU.mult))
            t4 = on_dve([t4], lambda e, _: e.tensor_scalar(v["dab"], v["dtv"], 0.0, None, ALU.max))
            t_dtf = on_dve([t4], lambda e, _: e.scalar_tensor_tensor(
                out=v["dt"], in0=v["dp"], scalar=2.0, in1=v["dab"], op0=ALU.mult, op1=ALU.add))
            t_av = on_dve([t_dtf], lambda e, _: e.tensor_tensor(
                sml["av"][:], sml["dt"][:], na[:].unsqueeze(1).to_broadcast([P, chunks, heads]), ALU.mult))
            t_ap = on_dve([t_av, sm_free], lambda e, _: e.tensor_copy(
                ap6[:], sml["av"][:].unsqueeze(2).to_broadcast([P, chunks, 6, heads])))
            t_c = project(banks[4], di + ns, ns)
            t_ct = on_act([t_c], lambda e, _: e.mul(ct, banks[4].buffer[:], unscale))
            banks[4].done(t_ct)
            free = banks[5].take()
            w = chunks * heads
            on_pe([free, t_av], lambda e, _: e.matmul(
                banks[5].buffer[:, 0:w], upp[:], v["av"], start=True, stop=True), mark=False)
            t_cs = on_pe([], lambda e, _: e.matmul(
                banks[5].buffer[:, w:2 * w], ones[:], v["av"], start=True, stop=True))
            free = banks[6].take()
            for c in range(chunks):
                t_cst = on_pe([free, t_ap], lambda e, _, c=c: e.matmul(
                    banks[6].buffer[0:cs_k, c * P:(c + 1) * P],
                    ap6[:, c, :, :].rearrange("p j h -> p (j h)"), upp[:],
                    start=True, stop=True), mark=(c == chunks - 1))
            t_e1 = on_act([t_cs, sm_free], lambda e, _: e.activation(v["ecs"], banks[5].buffer[:, 0:w], ACT.Exp))
            t_e2 = on_act([], lambda e, _: e.activation(v["dec"], banks[5].buffer[:, w:2 * w], ACT.Exp))
            t_e3 = on_dve([t_cs, t_e2, sm_free], lambda e, _: e.tensor_copy(v["cs"], banks[5].buffer[:, 0:w]))
            t_e3 = on_dve([t_e3], lambda e, _: e.tensor_tensor(
                v["cs"], banks[5].buffer[:, w:2 * w], v["cs"], ALU.subtract))
            banks[5].done(t_e1, t_e2, t_e3)
            t_e3 = on_act([t_e3], lambda e, _: e.activation(v["dst"], v["cs"], ACT.Exp))
            decays = [t_e1, t_e2, t_e3, t_dtf]
            free = full[0].take() + full[1].take() + edc[0].take()
            rest = full[0].buffer[0:cs_k, :]
            p1, p2 = (full[1].buffer[0:cs_k, n * tb // 2:(n + 1) * tb // 2].bitcast(BF16) for n in range(2))
            p3, pp = (edc[0].buffer[0:cs_k, n * tb // 2:(n + 1) * tb // 2].bitcast(BF16) for n in range(2))
            sums = banks[6].buffer[0:cs_k, :]
            t_f = on_dve([t_cst, free], lambda e, _: e.tensor_copy(p1, sums))
            t_q = on_dve([t_f], lambda e, _: e.tensor_scalar(pp, p1, csr[:, 0:1], None, ALU.mult))
            t_f = on_dve([t_f], lambda e, _: e.tensor_tensor(rest, sums, p1, ALU.subtract))
            banks[6].done(t_f)
            t_f = on_dve([t_f], lambda e, _: e.tensor_copy(p2, rest))
            t_q = on_dve([t_f, t_q], lambda e, _: e.scalar_tensor_tensor(
                out=pp, in0=p2, scalar=csr[:, 1:2], in1=pp, op0=ALU.mult, op1=ALU.add))
            t_f = on_dve([t_f], lambda e, _: e.tensor_tensor(p3, rest, p2, ALU.subtract))
            t_q = on_dve([t_f, t_q], lambda e, _: e.scalar_tensor_tensor(
                out=pp, in0=p3, scalar=csr[:, 2:3], in1=pp, op0=ALU.mult, op1=ALU.add))
            t_csq = on_dve([t_q, sm_free], lambda e, _: e.tensor_scalar(
                csq[:], pp, csr[:, 5:6], csr[:, 6:7], ALU.mult, ALU.add))
            t_lhs = on_dve([t_q, sm_free], lambda e, _: e.tensor_scalar(
                lhs_cs[:], pp, csr[:, 3:4], csr[:, 4:5], ALU.mult, ALU.add))
            for sl in (full[0], full[1], edc[0]):
                sl.done(t_lhs)

            free = banks[2].take()
            for c in range(chunks):
                t_t = on_pe([t_bt, free], lambda e, _, c=c: e.transpose(
                    banks[2].buffer[:, c * P:(c + 1) * P], bt[:, c * P:(c + 1) * P], idn[:]),
                    mark=(c == chunks - 1))
            t_bk = on_act([t_t], lambda e, _: e.copy(btok, banks[2].buffer[:]))
            banks[2].done(t_bk)
            free = banks[3].take()
            for c in range(chunks):
                t_g = on_pe([t_ct, t_bt, free], lambda e, _, c=c: e.matmul(
                    banks[3].buffer[:, c * P:(c + 1) * P], bt[:, c * P:(c + 1) * P],
                    ct[:, c * P:(c + 1) * P], start=True, stop=True), mark=(c == chunks - 1))
            g_free = gt_s.take()
            t_gt = on_act([t_g, g_free], lambda e, _: e.copy(gt[:].rearrange("p c t -> p (c t)"), banks[3].buffer[:]))
            banks[3].done(t_gt)

            def project_x(u):
                c, hf = units[u]
                bx = banks[0]
                free = bx.take()
                n = 0
                for k in range(ki):
                    for a, b in split_passes(s_parts, wx):
                        n += 1
                        t_x = on_pe([free, s_ready[k]], lambda e, _, k=k, a=a, b=b, n=n: e.matmul(
                            bx.buffer[:], a[:, k, c * P:(c + 1) * P], b[:, k, hf * half:(hf + 1) * half],
                            start=(n == 1), stop=(n == 3 * ki)), mark=(n == 3 * ki))
                x_ = xs[u % 2]
                x_free = x_.take()
                t_xs = on_act([t_x, x_free], lambda e, _: e.mul(x_.buffer[:], bx.buffer[:], unscale))
                bx.done(t_xs)
                h0 = hf * hph
                d_free, e_free, p_free = xdt.take(), xst.take(), xdp_s.take()
                t_xd = on_dve([t_xs, t_dtf, d_free], lambda e, _: e.tensor_tensor(
                    by_head(xdt.buffer[:], hd), by_head(x_.buffer[:], hd),
                    heads_over(sml["dt"][:, c, :], h0, hph, hd), ALU.mult))
                t_sk = on_pool([t_xd], lambda e, _: e.tensor_tensor(
                    by_head(x_.buffer[:], hd), by_head(x_.buffer[:], hd),
                    heads_over(dsk[:], h0, hph, hd), ALU.mult))
                t_xe = on_pool([t_xd, decays, e_free], lambda e, _: e.tensor_tensor(
                    by_head(xst.buffer[:], hd), by_head(xdt.buffer[:], hd),
                    heads_over(sml["dst"][:, c, :], h0, hph, hd), ALU.mult))
                t_hi = on_act([t_xd, p_free], lambda e, _: e.mul(xdp[0][:], xdt.buffer[:], XDT_SCALE))
                t_lo = on_dve([t_hi, p_free], lambda e, _: e.scalar_tensor_tensor(
                    out=xdp[1][:], in0=xdt.buffer[:], scalar=XDT_SCALE, in1=xdp[0][:],
                    op0=ALU.mult, op1=ALU.subtract))
                xdt.done(t_xe, t_lo)
                xes[u] = (x_, t_x, t_sk, t_xe, t_lo)

            spread = {}

            def spread_heads(u):
                if u >= len(units):
                    return
                c, hf = units[u]
                rhs = rhs_cs[u % 2]
                free = rhs.take()
                spread[u] = rhs, on_pool([t_csq, free], lambda e, _: e.tensor_tensor(
                    by_head(rhs.buffer[:], P),
                    csh[:, hf * hph:(hf + 1) * hph].unsqueeze(2).to_broadcast([cs_k, hph, P]),
                    csq[:, c * P:(c + 1) * P].unsqueeze(1).to_broadcast([cs_k, hph, P]), ALU.mult))

            def decay(u):
                c, hf = units[u]
                rhs, t_rhs = spread[u]
                out_ = []
                for g in range(hph // hpg):
                    bk, ed, md = banks[2 + g], edc[g], mdc[2 * (u % 2) + g]
                    free = bk.take()
                    on_pe([free, t_lhs, t_rhs], lambda e, _, g=g, bk=bk: e.matmul(
                        bk.buffer[:], lhs_cs[:, c * P:(c + 1) * P],
                        rhs.buffer[:, g * hpg * P:(g + 1) * hpg * P],
                        start=True, stop=False), mark=False)
                    t_a = on_pe([], lambda e, _, bk=bk: e.matmul(
                        bk.buffer[:], idb[:], neg[:], start=False, stop=True))
                    e_free, m_free = ed.take(), md.take()
                    t_e = on_act([t_a, e_free], lambda e, _, bk=bk, ed=ed: e.activation(
                        ed.buffer[:], bk.buffer[:], ACT.Exp))
                    bk.done(t_e)
                    t_m = on_dve([t_e, t_gt], lambda e, _, ed=ed: e.tensor_tensor(
                        by_head(ed.buffer[:], P), by_head(ed.buffer[:], P),
                        gt[:, c, :].unsqueeze(1).to_broadcast([P, hpg, P]), ALU.mult))
                    out_.append((ed, md, t_m, m_free))
                rhs.done(t_a)
                made = []
                for ed, md, t_m, m_free in out_:
                    t_hi = on_act([t_m, m_free], lambda e, _, ed=ed, md=md: e.mul(
                        md.buffer[:, 0, :], ed.buffer[:], M_SCALE))
                    made.append((md, on_dve([t_hi, m_free], lambda e, _, ed=ed, md=md: e.scalar_tensor_tensor(
                        out=md.buffer[:, 1, :], in0=ed.buffer[:], scalar=M_SCALE, in1=md.buffer[:, 0, :],
                        op0=ALU.mult, op1=ALU.subtract))))
                    ed.done(made[-1][1])
                return made, t_a

            def before_chunk(u):
                c, hf = units[u]
                b, h0, bo = c // (chunks // batches), hf * hph, banks[5]
                st = state[b][:, hf * half:(hf + 1) * half]
                free = bo.take()
                t_o = on_pe([free, state_ready[b][hf]], lambda e, _: e.matmul(
                    bo.buffer[:], ct[:, c * P:(c + 1) * P], st, start=True, stop=True))
                t_sd = on_pool([t_o, decays], lambda e, _: e.tensor_tensor(
                    by_head(st, hd), by_head(st, hd),
                    heads_over(sml["dec"][:, c, :], h0, hph, hd), ALU.mult))
                y_ = yac[u % 2]
                y_free = y_.take()
                t_1 = on_dve([t_o, decays, y_free], lambda e, _: e.tensor_tensor(
                    by_head(y_.buffer[:], hd), by_head(bo.buffer[:], hd),
                    heads_over(sml["ecs"][:, c, :], h0, hph, hd), ALU.mult))
                bo.done(t_1)
                return st, t_sd, y_, t_1

            def scan(u, mats, from_state):
                c, hf = units[u]
                b = c // (chunks // batches)
                st, t_sd, y_, t_1 = from_state
                x_, _, t_sk, t_xe, t_xp = xes[u]
                g_, t_gz = gates[u]
                by, bs = banks[4], banks[6]
                free = by.take()
                for h in range(hph):
                    md, t_m = mats[h // hpg]
                    for n, (a, v_) in enumerate(split_passes([md.buffer[:, q, :] for q in range(2)], xdp)):
                        t_y = on_pe([free, t_m, t_xp], lambda e, _, h=h, a=a, v_=v_, n=n: e.matmul(
                            by.buffer[:, h * hd:(h + 1) * hd], a[:, (h % hpg) * P:(h % hpg + 1) * P],
                            v_[:, h * hd:(h + 1) * hd], start=(n == 0), stop=(n == 2)),
                            mark=(h % hpg == hpg - 1 and n == 2))
                    if h % hpg == hpg - 1:
                        md.done(t_y)
                xdp_s.done(t_y)
                free = bs.take()
                t_s = on_pe([free, t_xe, t_bk], lambda e, _: e.matmul(
                    bs.buffer[:], btok[:, c * P:(c + 1) * P], xst.buffer[:], start=True, stop=True))
                xst.done(t_s)
                t_2 = on_pool([t_1, t_sk], lambda e, _: e.tensor_tensor(
                    y_.buffer[:], y_.buffer[:], x_.buffer[:], ALU.add))
                x_.done(t_2)
                t_3 = on_dve([t_2, t_y], lambda e, _: e.scalar_tensor_tensor(
                    out=y_.buffer[:], in0=by.buffer[:], scalar=1.0 / (M_SCALE * XDT_SCALE),
                    in1=y_.buffer[:], op0=ALU.mult, op1=ALU.add))
                by.done(t_3)
                t_sa = on_dve([t_sd, t_s], lambda e, _: e.tensor_tensor(st, bs.buffer[:], st, ALU.add))
                bs.done(t_sa)
                state_ready[b][hf] = [t_sa]
                t_4 = on_dve([t_3, t_gz], lambda e, _: e.tensor_tensor(
                    y_.buffer[:], y_.buffer[:], g_.buffer[:], ALU.mult))
                g_.done(t_4)
                return t_4, y_, (t_y, t_s)

            y_parts = {}

            def turn_y(u, t_4, y_):
                c, hf = units[u]
                bk = banks[7]
                free = bk.take()
                per = half // P
                for j in range(per):
                    t_t = on_pe([free, t_4], lambda e, _, j=j: e.transpose(
                        bk.buffer[:, j * P:(j + 1) * P], y_.buffer[:, j * P:(j + 1) * P], idn[:]),
                        mark=(j == per - 1))
                y_.done(t_t)
                ks = slice(hf * per, (hf + 1) * per)
                if hf == 0:
                    y_parts["free"], y_parts["ready"] = yt_s.take(), []
                src = bk.buffer[:].rearrange("p (k t) -> p k t", k=per)
                down = Y_SCALE / (2.0 * XN_SCALE * W_SCALE)
                t_hi = on_act([t_t, y_parts["free"]], lambda e, _: e.mul(yt[0][:, ks, :], src, down))
                t_lo = on_dve([t_hi, y_parts["free"]], lambda e, _: e.scalar_tensor_tensor(
                    out=yt[1][:, ks, :], in0=src, scalar=down, in1=yt[0][:, ks, :],
                    op0=ALU.mult, op1=ALU.subtract))
                bk.done(t_hi, t_lo)
                y_parts["ready"] += [t_hi, t_lo]

            attn = {}

            def project_out(c):
                bk = banks[7]
                free = bk.take()
                y_ready = y_parts["ready"]
                n = 0
                for k in range(ki):
                    for a, b in split_passes(yt, wo):
                        n += 1
                        t_p = on_pe([free, y_ready] if n == 1 else [], lambda e, _, k=k, a=a, b=b, n=n: e.matmul(
                            bk.buffer[:], a[:, k, :], b[:, k, :], start=(n == 1), stop=(n == 3 * ki)),
                            mark=(n == 3 * ki))
                yt_s.done(t_p)
                r = res[c]
                free = r.take()
                landed = load([free], lambda e, blk: e.dma_start(r.buffer[:], rows(x, c, blk)), st_res[c])
                t_r = on_dve([t_p, landed], lambda e, _: e.scalar_tensor_tensor(
                    out=r.buffer[:], in0=bk.buffer[:], scalar=1.0 / (Y_SCALE * W_SCALE), in1=r.buffer[:],
                    op0=ALU.mult, op1=ALU.add))
                bk.done(t_r)
                attn[c] = t_r

            state_ready = [[[state_made["loop"][b][hf]] if last else
                            [lambda b=b, hf=hf: [state_made["loop"][b][hf].before()]]
                            for hf in range(halves)] for b in range(batches)]
            spread_heads(0)
            spread_heads(1)
            project_x(0)
            project_z(1)
            mats, t_arg = decay(0)
            spread_heads(2)
            done_y = None
            for u in range(len(units)):
                here = mats
                old = before_chunk(u)
                if u:
                    turn_y(*done_y)
                if u + 1 < len(units):
                    mats, t_arg = decay(u + 1)
                t_4, y_, t_scan = scan(u, here, old)
                done_y = (u, t_4, y_)
                if u + 1 < len(units):
                    project_x(u + 1)
                if u and units[u - 1][1] == halves - 1:
                    project_out(units[u - 1][0])
                if u + 2 < len(units):
                    project_z(u + 2)
                spread_heads(u + 3)
            small_s.done(t_4, t_scan[0], t_arg)
            gt_s.done(t_4)
            state_made[pr.section] = [[state_ready[b][hf][0] for hf in range(halves)]
                                      for b in range(batches)]
            arena_s.done(xes[len(units) - 1][1])
            arena_b.done(*t_scan)

            s_free, b_free = arena_s.take(), arena_b.take()
            h_ready, mids = [], {}

            def ffn_up(m):
                ts = []
                for j in range(2):
                    bk = banks[2 * (m % 2) + j]
                    free = bk.take()
                    n = 0
                    for k in range(kd):
                        for part in xt:
                            n += 1
                            t = on_pe([free], lambda e, _, j=j, k=k, part=part, bk=bk, n=n: e.matmul(
                                bk.buffer[:], q12[:, j, k, m * P:(m + 1) * P], part[:, k, :],
                                start=(n == 1), stop=(n == 2 * kd)), mark=(n == 2 * kd), apart=True)
                    ts.append((t, bk))
                (t_1, b1), (t_2, b2) = ts
                th, fl = tnh[m % 2], full[m % 2]
                th_free, fl_free = th.take(), fl.take()
                t_th = on_act([t_1, th_free], lambda e, _: e.activation(
                    th.buffer[:], b1.buffer[:], ACT.Tanh, scale=0.5 / XN_SCALE))
                b1.done(t_th)
                t_f = on_dve([t_th, t_2, fl_free], lambda e, _: e.scalar_tensor_tensor(
                    out=fl.buffer[:], in0=th.buffer[:], scalar=1.0, in1=b2.buffer[:],
                    op0=ALU.add, op1=ALU.mult))
                b2.done(t_f)
                th.done(t_f)
                mids[m] = (fl, t_f)
                return t_2

            def ffn_parts(m):
                fl, t_f = mids[m]
                hid_free = [s_free, b_free if (m + 1) * 2 * tb > after_s else []]
                hid_free = hid_free[0] + hid_free[1]
                t_hi = on_act([t_f, hid_free], lambda e, _: e.copy(hid[:, m, 0, :], fl.buffer[:]))
                t_lo = on_dve([t_hi, hid_free], lambda e, _: e.tensor_tensor(
                    hid[:, m, 1, :], fl.buffer[:], hid[:, m, 0, :], ALU.subtract))
                fl.done(t_lo)
                h_ready.append(t_lo)

            between, x_tok = ([], []) if last else norm(1)
            for m in range(kf):
                if m:
                    ffn_parts(m - 1)
                t_2 = ffn_up(m)
                if m == 0:
                    turn_y(*done_y)
                if m == 1:
                    project_out(units[-1][0])
                if m >= 2 and between:
                    between.pop(0)()
            while between:
                between.pop(0)()
            if not last:
                xt_made["loop"] = turn(x_tok, t_2)
            ffn_parts(kf - 1)

            waiting = []

            def next_branch(m):
                if waiting:
                    n, *rest = waiting.pop()
                    branch_made[n]["loop"] = silu(n, *rest)
                if m < ki and not last:
                    waiting.append((m, *x_branch(m, xt_made["loop"])))

            for c in range(chunks):
                if c:
                    next_branch(2 * c - 2)
                bk = banks[c]
                free = bk.take()
                n = 0
                for m in range(kf):
                    for p in range(2):
                        n += 1
                        t_p = on_pe([free, h_ready[m]], lambda e, _, m=m, p=p, c=c, bk=bk, n=n: e.matmul(
                            bk.buffer[:], hid[:, m, p, c * P:(c + 1) * P], q3[:, m, :],
                            start=(n == 1), stop=(n == 2 * kf)), mark=(n == 2 * kf), apart=True)
                r = res[c]
                t_r = on_dve([t_p, attn[c]], lambda e, _, r=r, bk=bk: e.scalar_tensor_tensor(
                    out=r.buffer[:], in0=bk.buffer[:], scalar=1.0 / HID_SCALE, in1=r.buffer[:],
                    op0=ALU.mult, op1=ALU.add))
                bk.done(t_r)
                stored = load([t_r], lambda e, blk, r=r, c=c: e.dma_start(rows(out, c, blk), r.buffer[:]), st_out[c])
                r.done(stored)
                if c:
                    next_branch(2 * c - 1)
            next_branch(ki - 2)
            next_branch(ki - 1)
            next_branch(ki)
            arena_s.done(t_p)
            arena_b.done(t_p)

        xt_made, state_made = {}, {}
        branch_made = [{} for _ in range(ki)]
        engines = ("tensor", "scalar", "vector", "gpsimd", "sync")
        for name in engines:
            pr.step(name, set_up, lambda e, _: None)
        steps, x_tok = norm(0)
        for step in steps:
            step()
        xt_first = turn(x_tok, [])
        branch_first = []
        for m in range(ki + 1):
            if m:
                branch_first.append(silu(m - 1, *made))
            if m < ki:
                made = x_branch(m, xt_first, t_clear)
        pr.section = "loop"
        body(False)
        pr.section = "last"
        body(True)
        finals = [t for s in st_out for t in [Token(s, "last", s.counts["last"])]]
        pr.step("sync", finals, lambda e, _: None)

        credit = {"tensor": [pe], "scalar": [act], "vector": [dve], "gpsimd": [pool],
                  "sync": [*st_x, *st_res, *st_out]}
        block = ctx.enter_context(nc.Block())

        def emit(name):
            def run(eng):
                for s in credit[name]:
                    if s.counts["loop"]:
                        eng.sem_inc(s.sem["block"], s.counts["loop"])
                pr.play(name, eng, "setup", 0)
                with eng.Fori(0, nb - 1) as i:
                    pr.play(name, eng, "loop", i)
                pr.play(name, eng, "last", nb - 1)
            return run

        block.tensor(emit("tensor"))
        block.scalar(emit("scalar"))
        block.vector(emit("vector"))
        block.gpsimd(emit("gpsimd"))
        block.sync(emit("sync"))


def kernel(**inputs):
    import concourse.bacc as bacc
    from concourse.bass_utils import run_bass_kernel_spmd

    def get(name):
        return np.asarray(inputs[name])

    def tiles(w):
        n, k = w.shape
        return np.ascontiguousarray(w.T.reshape(k // P, P, n).transpose(1, 0, 2).reshape(P, -1))

    heads = 16
    w_x = get("L0_attn_x_proj_w")
    di = w_x.shape[1]
    cw = get("L0_attn_conv_w")
    ki = cw.shape[0] // P
    bf16 = np.dtype("bfloat16")
    s_, l_ = np.arange(P)[:, None], np.arange(P)[None, :]
    mask_neg = np.tile(np.where(l_ < s_, -1e30, 0.0), (1, 4)).astype(bf16)
    upper = (s_ <= l_).astype(np.float32)
    row = np.arange(6 * heads)
    part, second = row // heads % 3, row >= 3 * heads
    cs_rows = np.stack([part == 0, part == 1, part == 2, -1.0 * ~second, second, second, ~second],
                       axis=1).astype(np.float32)
    cs_heads = (row[:, None] % heads == np.arange(heads)).astype(bf16)
    arrays = {
        "x": get("L0_attn_x"),
        "w_in": np.ascontiguousarray(get("L0_attn_in_proj_w").T),
        "conv_w": np.ascontiguousarray(cw.reshape(ki, P, -1).transpose(1, 0, 2)),
        "conv_b": np.ascontiguousarray(get("L0_attn_conv_b").reshape(ki, P).T),
        "w_x": np.ascontiguousarray(np.concatenate([w_x[:di], w_x[di + heads:]]).T),
        "w_xdt": np.ascontiguousarray(w_x[di:di + heads]),
        "w_dt": np.ascontiguousarray(get("L0_attn_dt_proj_w").T),
        "dt_bias": get("L0_attn_dt_proj_b"),
        "a_log": get("L0_attn_A_log"),
        "d_skip": get("L0_attn_D"),
        "w_out": np.ascontiguousarray(get("L0_attn_out_proj_w").T),
        "w_ffn": np.concatenate([tiles(get(f"L0_ffn_w{n}")) for n in (1, 2, 3)], axis=1),
        "ident": np.eye(P, dtype=np.float32),
        "mask_neg": mask_neg,
        "upper": upper,
        "cs_rows": cs_rows,
        "cs_heads": cs_heads,
    }
    nc = bacc.Bacc("TRN2", target_bir_lowering=False, num_devices=1, dynamic_dma_scratch_size=1024)
    args = [nc.dram_tensor(n, a.shape, mybir.dt.from_np(a.dtype), kind="ExternalInput").ap()
            for n, a in arrays.items()]
    out = nc.dram_tensor("out", arrays["x"].shape, F32, kind="ExternalOutput").ap()
    mamba_ffn_block(nc, *args, out)
    return run_bass_kernel_spmd(nc, [arrays], core_ids=[0]).results[0]["out"]
```

```python
from contextlib import ExitStack

import numpy as np

import concourse.bass as bass
from concourse import mybir

ACT = mybir.ActivationFunctionType
ALU = mybir.AluOpType
F32 = mybir.dt.float32
F16 = mybir.dt.float16
BF16 = mybir.dt.bfloat16
FP8 = mybir.dt.float8e4

P = 128
DMA = 16

XN_SCALE = 2.0 ** 5
W_SCALE = 2.0 ** 8
CONV_SCALE = 2.0 ** 7
S_SCALE = 2.0 * CONV_SCALE
Y_SCALE = 2.0 ** 10
XDT_SCALE = 2.0 ** 10
M_SCALE = 2.0 ** 6
HID_SCALE = 2.0 * XN_SCALE
ROUND = 1.5 * 2.0 ** 23


class Token:

    def __init__(self, stream, section, count):
        self.stream, self.section, self.count = stream, section, count


class Stream:

    def __init__(self, name, setup_sem, block_sem, step=1):
        self.name, self.sem, self.step = name, {"setup": setup_sem, "block": block_sem}, step
        self.counts = {"setup": 0, "first": 0, "loop": 0, "last": 0}

    def mark(self, section):
        self.counts[section] += self.step
        return Token(self, section, self.counts[section])


class Program:

    def __init__(self):
        self.queues = {}
        self.section = "setup"
        self.aside = False

    def step(self, engine, waits, issue, stream=None, apart=False):
        token = stream.mark("setup" if self.aside else self.section) if stream else None
        flat = []
        for w in waits:
            flat += w if isinstance(w, (list, tuple)) else [w]
        self.queues.setdefault((engine, self.section), []).append((flat, issue, token, apart))
        return token

    def play(self, engine, handle, section, block):
        reached = {}
        for waits, issue, token, apart in self.queues.get((engine, section), []):
            waited = False
            for t in waits:
                per = t.stream.counts["loop"]
                if t.section == "setup":
                    kind, level, value = "setup", t.count, t.count
                else:
                    kind = "block"
                    back = 0 if t.section == section else 1
                    level = t.count - back * per
                    value = block * per + level
                if reached.get((t.stream.name, kind), -10 ** 9) >= level:
                    continue
                reached[t.stream.name, kind] = level
                handle.wait_ge(t.stream.sem[kind], value)
                waited = waited or kind == "block"
            if issue is None:
                continue
            if apart and waited:
                handle.sem_inc(self.passed, 1)
            made = issue(handle, block)
            if token is not None:
                kind = "setup" if token.section == "setup" else "block"
                made.then_inc(token.stream.sem[kind], token.stream.step)


class Slot:

    def __init__(self, program, buffer=None):
        self.program, self.buffer = program, buffer
        self.readers = []

    def take(self):
        assert self.readers is not None, "taken before its last user's readers are known"
        free, self.readers = self.readers, None
        return free

    def done(self, *tokens):
        self.readers = (self.readers or []) + list(tokens)


def mamba_ffn_block(nc, x, w_in, conv_w, conv_b, w_x, w_xdt, w_dt, dt_bias, a_log, d_skip, w_out,
                    w_ffn, ident, upper, cs_rows, cs_heads, out):
    batches, seqlen, dm = x.shape
    di = w_in.shape[1] // 2
    heads = w_dt.shape[0]
    hd = di // heads
    ns = (w_x.shape[1] - di) // 2
    fh = (w_ffn.shape[1]) // (3 * dm) * P
    tb = 512
    nb = batches * seqlen // tb
    span = tb // batches
    chunks = tb // P
    kd, ki, kf = dm // P, di // P, fh // P
    taps = conv_w.shape[2]
    halo = taps - 1
    half = 512
    halves = di // half
    hph = half // hd
    hpg = half // P
    assert batches == 2 and ns == P and chunks == 4 and dm == half and heads == 16

    pr = Program()
    ctx = ExitStack()
    with ctx:
        def sem(name):
            return ctx.enter_context(nc.semaphore(name))

        pr.passed = sem("passed")

        def stream(name, step=1):
            return Stream(name, sem(name + "_setup"), sem(name + "_blocks"), step)

        def sb(name, shape, dt=F32, where=ctx):
            return where.enter_context(nc.sbuf_tensor(name, shape, dt))

        pe, act, dve, pool = (stream(n) for n in ("pe", "act", "dve", "pool"))
        st_x = [stream(f"x_in{n}", DMA) for n in range(4)]
        st_res = [stream(f"residual{c}", DMA) for c in range(chunks)]
        st_out = [stream(f"stored{c}", DMA) for c in range(chunks)]
        streams = [pe, act, dve, pool, *st_x, *st_res, *st_out]

        def on_pe(waits, issue, mark=True, apart=False):
            return pr.step("tensor", waits, issue, pe if mark else None, apart)

        def on_act(waits, issue):
            return pr.step("scalar", waits, issue, act)

        def on_dve(waits, issue, apart=False):
            return pr.step("vector", waits, issue, dve, apart)

        def on_pool(waits, issue, apart=False):
            return pr.step("gpsimd", waits, issue, pool, apart)

        def load(waits, issue, st):
            return pr.step("sync", waits, issue, st)

        win = [sb(f"win_{p}", [P, kd, 2 * di], F16) for p in ("hi", "lo")]
        wx = [sb(f"wx_{p}", [P, ki, w_x.shape[1]], F16) for p in ("hi", "lo")]
        wo = [sb(f"wo_{p}", [P, ki, dm], F16) for p in ("hi", "lo")]
        q12 = sb("q12", [P, 2, kd, fh], FP8)
        q3 = sb("q3", [P, kf, dm], FP8)
        idn = sb("idn", [P, P])
        upp = sb("upp", [P, P])
        ones = sb("ones", [P, P])
        csr = sb("csr", list(cs_rows.shape))
        csh = sb("csh", list(cs_heads.shape), BF16)
        cw = sb("cw", [P, ki, taps])
        cws = sb("cws", [P, ki])
        cb = sb("cb", [P, ki])
        w2 = [sb(f"w2_{p}", [P, ki, heads], F16) for p in ("hi", "lo")]
        dtb = sb("dtb", [P, heads])
        na = sb("na", [P, heads])
        dsk = sb("dsk", [P, heads])
        mhalf = sb("mhalf", [P, chunks])
        state = [sb(f"state{b}", [P, di]) for b in range(batches)]
        hal = sb("hal", [P, ki, batches, halo])

        banks = [Slot(pr, ctx.enter_context(nc.psum_tensor(f"bank{n}", [P, half], F32)))
                 for n in range(8)]

        stats = sb("stats", [P, chunks, 6])
        mv = sb("mv", [P, chunks, 2])
        rstd = sb("rstd", [P, chunks])
        rstd_s = Slot(pr)
        xt = [sb(f"xt_{p}", [P, kd, tb], F16) for p in ("hi", "lo")]
        raw = [Slot(pr, sb(f"raw{n}", [P, batches, halo + span])) for n in range(2)]
        tnh = [Slot(pr, sb(f"tnh{n}", [P, tb])) for n in range(2)]
        full = [Slot(pr, sb(f"full{n}", [P, tb])) for n in range(2)]
        arena = sb("arena", [P, 2 * kf * tb], F16)
        s_parts = [arena[:, p * ki * tb:(p + 1) * ki * tb].rearrange("p (k t) -> p k t", k=ki)
                   for p in range(2)]
        after_s = 2 * ki * tb
        bt = arena[:, after_s:after_s + 2 * tb].bitcast(F32)
        ct = arena[:, after_s + 2 * tb:after_s + 4 * tb].bitcast(F32)
        btok = arena[:, after_s + 4 * tb:after_s + 6 * tb].bitcast(F32)
        hid = arena[:].rearrange("p (k q t) -> p k q t", k=kf, q=2)
        arena_s, arena_b = Slot(pr), Slot(pr)
        gt = sb("gt", [P, chunks, P])
        gt_s = Slot(pr)
        sml = {n: sb(n, [P, chunks, heads]) for n in
               ("dtv", "dab", "du", "dz", "dq", "dp", "dt", "av", "cs", "ecs", "dst", "dec")}
        cs_k = 6 * heads
        ap6 = sb("ap6", [P, chunks, 6, heads])
        lhs_cs = sb("lhs_cs", [cs_k, tb], BF16)
        csq = sb("csq", [cs_k, tb], BF16)
        rhs_cs = [Slot(pr, sb(f"rhs_cs{n}", [cs_k, hph * P], BF16)) for n in range(2)]
        small_s = Slot(pr)
        xs = [Slot(pr, sb(f"xs{n}", [P, half])) for n in range(2)]
        xdt = Slot(pr, sb("xdt", [P, half]))
        xdp = [sb(f"xdt_{p}", [P, half], F16) for p in ("hi", "lo")]
        xdp_s = Slot(pr)
        xst = Slot(pr, sb("xst", [P, half]))
        yac = [Slot(pr, sb(f"yac{n}", [P, half])) for n in range(2)]
        gate = [Slot(pr, sb(f"gate{n}", [P, half])) for n in range(2)]
        xin = [*yac, *gate]
        edc = [Slot(pr, sb(f"edc{n}", [P, hpg * P])) for n in range(2)]
        mdc = [Slot(pr, sb(f"mdc{n}", [P, 2, hpg * P], F16)) for n in range(4)]
        branch = [(sl, sl.buffer[:]) for sl in (*edc, *xs)]
        branch += [(sl, sl.buffer[:].rearrange("p q t -> p (q t)").bitcast(F32)) for sl in mdc]
        yt = [sb(f"yt_{p}", [P, ki, P], F16) for p in ("hi", "lo")]
        yt_s = Slot(pr)
        res = [Slot(pr, sb(f"res{c}", [P, dm])) for c in range(chunks)]

        def heads_over(v, h0, n, width):
            return v[:, h0:h0 + n].unsqueeze(2).to_broadcast([P, n, width])

        def by_head(v, width):
            return v.rearrange("p (h d) -> p h d", d=width)

        def rows(dram, c, block):
            b, at = c // (chunks // batches), (c % (chunks // batches)) * P
            if isinstance(block, int):
                return dram[b, block * span + at:block * span + at + P, :]
            return dram[b, bass.ds(block * span + at, P), :]

        def split_passes(a, b):
            return [(a[0], b[0]), (a[0], b[1]), (a[1], b[0])]

        def norm(shift, half_set=()):
            x_tok, seen = [], {}

            def statistics(c):
                if c == 0:
                    seen["free"] = rstd_s.take()
                s = xin[c]
                free = s.take()
                landed = load([free], lambda e, blk: e.dma_start(
                    s.buffer[:], rows(x, c, blk + shift)), st_x[c])
                t = on_dve([landed, seen["free"]], lambda e, _: e.bn_stats(stats[:, c, :], s.buffer[:]))
                seen["mv", c] = on_dve([t], lambda e, _: e.bn_aggr(mv[:, c, :], stats[:, c, :]), apart=True)

            def root():
                t = on_dve([seen["mv", chunks - 1]], lambda e, _: e.tensor_scalar(
                    rstd[:], mv[:, :, 1], 1e-5, None, ALU.add))
                t = on_pool([t, half_set], lambda e, _: e.tensor_tensor(rstd[:], rstd[:], mhalf[:], ALU.pow))
                seen["root"] = on_dve([t], lambda e, _: e.tensor_scalar(
                    rstd[:], rstd[:], XN_SCALE, None, ALU.mult))

            def normalise(c):
                s = xin[c]
                t = on_dve([seen["root"]], lambda e, _: e.tensor_scalar(
                    s.buffer[:], s.buffer[:], mv[:, c, 0:1], rstd[:, c:c + 1], ALU.subtract, ALU.mult))
                x_tok.append(t)
                if c == chunks - 1:
                    rstd_s.done(t)

            steps = [lambda c=c: statistics(c) for c in range(chunks)]
            steps += [root] + [lambda c=c: normalise(c) for c in range(chunks)]
            return steps, x_tok

        def turn(x_tok, xt_free):
            for k in range(kd):
                bk = banks[4 + k]
                free = bk.take()
                for c in range(chunks):
                    t_t = on_pe([free, x_tok[c], t_idn], lambda e, _, k=k, c=c, bk=bk: e.transpose(
                        bk.buffer[:, c * P:(c + 1) * P], xin[c].buffer[:, k * P:(k + 1) * P], idn[:]),
                        mark=(c == chunks - 1))
                t_hi = on_act([t_t, xt_free], lambda e, _, k=k, bk=bk: e.copy(xt[0][:, k, :], bk.buffer[:]))
                t_lo = on_dve([t_hi, xt_free], lambda e, _, k=k, bk=bk: e.tensor_tensor(
                    xt[1][:, k, :], bk.buffer[:], xt[0][:, k, :], ALU.subtract))
                bk.done(t_hi, t_lo)
            for s in xin:
                s.done(t_t)
            return t_lo

        def x_branch(m, xt_ready, cleared=()):
            bk = banks[4 + m % 4]
            free = bk.take()
            n = 0
            for k in range(kd):
                for a, b in split_passes(win, xt):
                    n += 1
                    t_mm = on_pe([free, xt_ready] if n == 1 else [],
                                 lambda e, _, k=k, a=a, b=b, n=n: e.matmul(
                                     bk.buffer[:], a[:, k, m * P:(m + 1) * P], b[:, k, :],
                                     start=(n == 1), stop=(n == 3 * kd)),
                                 mark=(n == 3 * kd))
            r, (a_, ab), tp = raw[m % 2], branch[m], (xdt, xst)[m % 2]
            r_free, a_free, p_free = r.take(), a_.take(), tp.take()
            acc3 = ab.rearrange("p (b t) -> p b t", b=batches)
            tp3 = tp.buffer[:].rearrange("p (b t) -> p b t", b=batches)
            t_h = on_pool([r_free, cleared], lambda e, _: e.tensor_copy(
                r.buffer[:, :, 0:halo], hal[:, m, :, :]), apart=True)
            t_raw = on_act([t_mm, r_free], lambda e, _: e.activation(
                r.buffer[:, :, halo:], bk.buffer[:].rearrange("p (b t) -> p b t", b=batches),
                ACT.Copy, scale=1.0 / (XN_SCALE * W_SCALE)))
            t_acc = on_act([a_free], lambda e, _: e.activation(
                ab, bk.buffer[:], ACT.Identity, scale=cws[:, m:m + 1], bias=cb[:, m:m + 1]))
            bk.done(t_acc)
            t_h2 = on_pool([t_h, t_raw], lambda e, _: e.tensor_copy(
                hal[:, m, :, :], r.buffer[:, :, span:span + halo]), apart=True)
            t_tap = on_act([t_h, t_raw, p_free], lambda e, _: e.mul(
                tp3, r.buffer[:, :, halo - 1:halo - 1 + span], cw[:, m, halo - 1:halo]))
            t_c = on_pool([t_acc, t_tap], lambda e, _: e.tensor_tensor(
                ab, ab, tp.buffer[:], ALU.add))
            tp.done(t_c)
            for j in range(halo - 1):
                t_c = on_dve([t_c, t_h2], lambda e, _, j=j: e.scalar_tensor_tensor(
                    out=acc3, in0=r.buffer[:, :, j:j + span],
                    scalar=cw[:, m, j:j + 1], in1=acc3, op0=ALU.mult, op1=ALU.add))
            r.done(t_c, t_h2, t_tap)
            return a_, ab, t_c

        def silu(m, a_, ab, t_c):
            th = tnh[m % 2]
            th_free = th.take()
            t_th = on_act([t_c, th_free], lambda e, _: e.activation(
                th.buffer[:], ab, ACT.Tanh, scale=0.5 / CONV_SCALE))
            t_f = on_dve([t_th], lambda e, _: e.scalar_tensor_tensor(
                out=ab, in0=th.buffer[:], scalar=1.0, in1=ab, op0=ALU.add, op1=ALU.mult))
            th.done(t_f)
            made["branch", m] = t_f

        made = {}

        def body(first, last):
            def aside(*counts):
                if first:
                    pr.aside = True
                    for _ in range(sum(counts)):
                        after.append(preparation.pop(0)())
                        rest = after.pop(0)
                        if rest:
                            rest()
                    pr.aside = False

            def weights_ready(name):
                if first:
                    pr.step("tensor", prepared[name], None)

            xt_ready = [made["xt"]]
            s_free, b_free = arena_s.take(), arena_b.take()
            s_ready = []

            def branch_parts(m):
                a_, ab = branch[m]
                t_f = made["branch", m]
                t_hi = on_act([t_f, s_free], lambda e, _: e.copy(s_parts[0][:, m, :], ab))
                t_lo = on_dve([t_f, t_hi, s_free], lambda e, _: e.tensor_tensor(
                    s_parts[1][:, m, :], ab, s_parts[0][:, m, :], ALU.subtract))
                a_.done(t_hi, t_lo)
                s_ready.append(t_lo)

            for m in range(ki):
                branch_parts(m)

            order = [0, 2, 1, 3]
            units = [(c, hf) for c in order for hf in range(halves)]
            gates, xes = {}, {}

            def project_z(u):
                c, hf = units[u]
                bz = banks[1]
                free = bz.take()
                n = 0
                for k in range(kd):
                    for a, b in split_passes(xt, win):
                        n += 1
                        t_z = on_pe([free, xt_ready], lambda e, _, k=k, a=a, b=b, n=n: e.matmul(
                            bz.buffer[:], a[:, k, c * P:(c + 1) * P],
                            b[:, k, di + hf * half:di + (hf + 1) * half],
                            start=(n == 1), stop=(n == 3 * kd)), mark=(n == 3 * kd))
                g_, th = gate[u % 2], tnh[u % 2]
                g_free, th_free = g_.take(), th.take()
                t_th = on_act([t_z, th_free], lambda e, _: e.activation(
                    th.buffer[:], bz.buffer[:], ACT.Tanh, scale=0.5 / (XN_SCALE * W_SCALE)))
                t_gz = on_dve([t_th, g_free], lambda e, _: e.scalar_tensor_tensor(
                    out=g_.buffer[:], in0=th.buffer[:], scalar=1.0, in1=bz.buffer[:],
                    op0=ALU.add, op1=ALU.mult))
                bz.done(t_gz)
                th.done(t_gz)
                gates[u] = (g_, t_gz)

            project_z(0)
            weights_ready("w_x")
            aside(4)

            def project(bk, col, width):
                free = bk.take()
                n = 0
                for k in range(ki):
                    for a, b in split_passes(wx, s_parts):
                        n += 1
                        t = on_pe([free, s_ready[k]], lambda e, _, k=k, a=a, b=b, n=n: e.matmul(
                            bk.buffer[0:width, :], a[:, k, col:col + width], b[:, k, :],
                            start=(n == 1), stop=(n == 3 * ki)), mark=(n == 3 * ki))
                return t

            unscale = 1.0 / (S_SCALE * W_SCALE)
            t_b = project(banks[3], di, ns)
            aside(4)
            t_bt = on_act([t_b, b_free], lambda e, _: e.mul(bt, banks[3].buffer[:], unscale))
            banks[3].done(t_bt)
            sm_free = small_s.take()
            free = banks[2].take()
            for c in range(chunks):
                n = 0
                for k in range(ki):
                    for a, b in split_passes(s_parts, w2):
                        n += 1
                        t_dp = on_pe([free, s_ready[k]], lambda e, _, c=c, k=k, a=a, b=b, n=n: e.matmul(
                            banks[2].buffer[:, c * heads:(c + 1) * heads], a[:, k, c * P:(c + 1) * P],
                            b[:, k, :], start=(n == 1), stop=(n == 3 * ki)),
                            mark=(c == chunks - 1 and n == 3 * ki))
            v = {n: t[:].rearrange("p c h -> p (c h)") for n, t in sml.items()}
            t1 = on_dve([t_dp, sm_free], lambda e, _: e.scalar_tensor_tensor(
                out=sml["dtv"][:], scalar=unscale, op0=ALU.mult, op1=ALU.add,
                in0=banks[2].buffer[:, 0:chunks * heads].rearrange("p (c h) -> p c h", h=heads),
                in1=dtb[:].unsqueeze(1).to_broadcast([P, chunks, heads])))
            banks[2].done(t1)
            t2 = on_dve([t1], lambda e, _: e.scalar_tensor_tensor(
                out=v["dab"], in0=v["dtv"], scalar=-1.0, in1=v["dtv"], op0=ALU.mult, op1=ALU.max))
            t3 = on_act([t2], lambda e, _: e.activation(v["du"], v["dab"], ACT.Exp, scale=-1.0))
            t4 = on_dve([t3], lambda e, _: e.tensor_scalar(v["dab"], v["du"], 2.0, None, ALU.add))
            t4 = on_dve([t4], lambda e, _: e.reciprocal(v["dz"], v["dab"]))
            t4 = on_dve([t4], lambda e, _: e.tensor_tensor(v["dz"], v["dz"], v["du"], ALU.mult))
            t4 = on_dve([t4], lambda e, _: e.tensor_tensor(v["dq"], v["dz"], v["dz"], ALU.mult))
            t4 = on_dve([t4], lambda e, _: e.tensor_scalar(v["dp"], v["dq"], 1.0 / 17, None, ALU.mult))
            for odd in range(15, 1, -2):
                t4 = on_dve([t4], lambda e, _, odd=odd: e.scalar_tensor_tensor(
                    out=v["dp"], in0=v["dp"], scalar=1.0 / odd, in1=v["dq"], op0=ALU.add, op1=ALU.mult))
            t4 = on_dve([t4], lambda e, _: e.scalar_tensor_tensor(
                out=v["dp"], in0=v["dp"], scalar=1.0, in1=v["dz"], op0=ALU.add, op1=ALU.mult))
            t4 = on_dve([t4], lambda e, _: e.tensor_scalar(v["dab"], v["dtv"], 0.0, None, ALU.max))
            t_dtf = on_dve([t4], lambda e, _: e.scalar_tensor_tensor(
                out=v["dt"], in0=v["dp"], scalar=2.0, in1=v["dab"], op0=ALU.mult, op1=ALU.add))
            t_av = on_dve([t_dtf], lambda e, _: e.tensor_tensor(
                sml["av"][:], sml["dt"][:], na[:].unsqueeze(1).to_broadcast([P, chunks, heads]), ALU.mult))
            t_ap = on_dve([t_av, sm_free], lambda e, _: e.tensor_copy(
                ap6[:], sml["av"][:].unsqueeze(2).to_broadcast([P, chunks, 6, heads])))
            aside(4)
            t_c = project(banks[4], di + ns, ns)
            t_ct = on_act([t_c], lambda e, _: e.mul(ct, banks[4].buffer[:], unscale))
            banks[4].done(t_ct)
            free = banks[5].take()
            w = chunks * heads
            on_pe([free, t_av], lambda e, _: e.matmul(
                banks[5].buffer[:, 0:w], upp[:], v["av"], start=True, stop=True), mark=False)
            t_cs = on_pe([], lambda e, _: e.matmul(
                banks[5].buffer[:, w:2 * w], ones[:], v["av"], start=True, stop=True))
            free = banks[6].take()
            for c in range(chunks):
                t_cst = on_pe([free, t_ap], lambda e, _, c=c: e.matmul(
                    banks[6].buffer[0:cs_k, c * P:(c + 1) * P],
                    ap6[:, c, :, :].rearrange("p j h -> p (j h)"), upp[:],
                    start=True, stop=True), mark=(c == chunks - 1))
            t_e1 = on_act([t_cs, sm_free], lambda e, _: e.activation(v["ecs"], banks[5].buffer[:, 0:w], ACT.Exp))
            t_e2 = on_act([], lambda e, _: e.activation(v["dec"], banks[5].buffer[:, w:2 * w], ACT.Exp))
            t_e3 = on_dve([t_cs, t_e2, sm_free], lambda e, _: e.tensor_copy(v["cs"], banks[5].buffer[:, 0:w]))
            t_e3 = on_dve([t_e3], lambda e, _: e.tensor_tensor(
                v["cs"], banks[5].buffer[:, w:2 * w], v["cs"], ALU.subtract))
            banks[5].done(t_e1, t_e2, t_e3)
            t_e3 = on_act([t_e3], lambda e, _: e.activation(v["dst"], v["cs"], ACT.Exp))
            decays = [t_e1, t_e2, t_e3, t_dtf]
            free = full[0].take() + full[1].take() + edc[0].take()
            rest = full[0].buffer[0:cs_k, :]
            p1, p2 = (full[1].buffer[0:cs_k, n * tb // 2:(n + 1) * tb // 2].bitcast(BF16) for n in range(2))
            p3, pp = (edc[0].buffer[0:cs_k, n * tb // 2:(n + 1) * tb // 2].bitcast(BF16) for n in range(2))
            sums = banks[6].buffer[0:cs_k, :]
            t_f = on_dve([t_cst, free], lambda e, _: e.tensor_copy(p1, sums))
            t_q = on_dve([t_f], lambda e, _: e.tensor_scalar(pp, p1, csr[:, 0:1], None, ALU.mult))
            t_f = on_dve([t_f], lambda e, _: e.tensor_tensor(rest, sums, p1, ALU.subtract))
            banks[6].done(t_f)
            t_f = on_dve([t_f], lambda e, _: e.tensor_copy(p2, rest))
            t_q = on_dve([t_f, t_q], lambda e, _: e.scalar_tensor_tensor(
                out=pp, in0=p2, scalar=csr[:, 1:2], in1=pp, op0=ALU.mult, op1=ALU.add))
            t_f = on_dve([t_f], lambda e, _: e.tensor_tensor(p3, rest, p2, ALU.subtract))
            t_q = on_dve([t_f, t_q], lambda e, _: e.scalar_tensor_tensor(
                out=pp, in0=p3, scalar=csr[:, 2:3], in1=pp, op0=ALU.mult, op1=ALU.add))
            t_csq = on_dve([t_q, sm_free], lambda e, _: e.tensor_scalar(
                csq[:], pp, csr[:, 5:6], csr[:, 6:7], ALU.mult, ALU.add))
            t_lhs = on_dve([t_q, sm_free], lambda e, _: e.tensor_scalar(
                lhs_cs[:], pp, csr[:, 3:4], csr[:, 4:5], ALU.mult, ALU.add))
            for sl in (full[0], full[1], edc[0]):
                sl.done(t_lhs)

            free = banks[2].take()
            for c in range(chunks):
                t_t = on_pe([t_bt, free], lambda e, _, c=c: e.transpose(
                    banks[2].buffer[:, c * P:(c + 1) * P], bt[:, c * P:(c + 1) * P], idn[:]),
                    mark=(c == chunks - 1))
            t_bk = on_act([t_t], lambda e, _: e.copy(btok, banks[2].buffer[:]))
            banks[2].done(t_bk)
            free = banks[3].take()
            for c in range(chunks):
                t_g = on_pe([t_ct, t_bt, free], lambda e, _, c=c: e.matmul(
                    banks[3].buffer[:, c * P:(c + 1) * P], bt[:, c * P:(c + 1) * P],
                    ct[:, c * P:(c + 1) * P], start=True, stop=True), mark=(c == chunks - 1))
            g_free = gt_s.take()
            t_gt = on_dve([t_g, g_free], lambda e, _: e.tensor_tensor(
                gt[:], by_head(banks[3].buffer[:], P), upp[:].unsqueeze(1).to_broadcast([P, chunks, P]),
                ALU.mult))
            banks[3].done(t_gt)

            def project_x(u):
                c, hf = units[u]
                bx = banks[0]
                free = bx.take()
                n = 0
                for k in range(ki):
                    for a, b in split_passes(s_parts, wx):
                        n += 1
                        t_x = on_pe([free, s_ready[k]], lambda e, _, k=k, a=a, b=b, n=n: e.matmul(
                            bx.buffer[:], a[:, k, c * P:(c + 1) * P], b[:, k, hf * half:(hf + 1) * half],
                            start=(n == 1), stop=(n == 3 * ki)), mark=(n == 3 * ki))
                x_ = xs[u % 2]
                x_free = x_.take()
                t_xs = on_act([t_x, x_free], lambda e, _: e.mul(x_.buffer[:], bx.buffer[:], unscale))
                bx.done(t_xs)
                h0 = hf * hph
                d_free, e_free, p_free = xdt.take(), xst.take(), xdp_s.take()
                t_xd = on_dve([t_xs, t_dtf, d_free], lambda e, _: e.tensor_tensor(
                    by_head(xdt.buffer[:], hd), by_head(x_.buffer[:], hd),
                    heads_over(sml["dt"][:, c, :], h0, hph, hd), ALU.mult))
                t_sk = on_pool([t_xd], lambda e, _: e.tensor_tensor(
                    by_head(x_.buffer[:], hd), by_head(x_.buffer[:], hd),
                    heads_over(dsk[:], h0, hph, hd), ALU.mult))
                t_xe = on_pool([t_xd, decays, e_free], lambda e, _: e.tensor_tensor(
                    by_head(xst.buffer[:], hd), by_head(xdt.buffer[:], hd),
                    heads_over(sml["dst"][:, c, :], h0, hph, hd), ALU.mult))
                t_hi = on_act([t_xd, p_free], lambda e, _: e.mul(xdp[0][:], xdt.buffer[:], XDT_SCALE))
                t_lo = on_dve([t_hi, p_free], lambda e, _: e.scalar_tensor_tensor(
                    out=xdp[1][:], in0=xdt.buffer[:], scalar=XDT_SCALE, in1=xdp[0][:],
                    op0=ALU.mult, op1=ALU.subtract))
                xdt.done(t_xe, t_lo)
                xes[u] = (x_, t_x, t_sk, t_xe, t_lo)

            spread = {}

            def spread_heads(u):
                if u >= len(units):
                    return
                c, hf = units[u]
                rhs = rhs_cs[u % 2]
                free = rhs.take()
                spread[u] = rhs, on_pool([t_csq, free], lambda e, _: e.tensor_tensor(
                    by_head(rhs.buffer[:], P),
                    csh[:, hf * hph:(hf + 1) * hph].unsqueeze(2).to_broadcast([cs_k, hph, P]),
                    csq[:, c * P:(c + 1) * P].unsqueeze(1).to_broadcast([cs_k, hph, P]), ALU.mult))

            def decay(u):
                c, hf = units[u]
                rhs, t_rhs = spread[u]
                out_, mid = [], []
                for g in range(hph // hpg):
                    bk, ed, md = banks[2 + g], edc[g], mdc[2 * (u % 2) + g]
                    free = bk.take()
                    t_a = on_pe([free, t_lhs, t_rhs], lambda e, _, g=g, bk=bk: e.matmul(
                        bk.buffer[:], lhs_cs[:, c * P:(c + 1) * P],
                        rhs.buffer[:, g * hpg * P:(g + 1) * hpg * P],
                        start=True, stop=True))
                    e_free, m_free = ed.take(), md.take()
                    t_e = on_act([t_a, e_free], lambda e, _, bk=bk, ed=ed: e.activation(
                        ed.buffer[:], bk.buffer[:], ACT.Relu, scale=-1.0))
                    bk.done(t_e)
                    mid.append((ed, md, t_e, m_free))
                for ed, md, t_e, m_free in mid:
                    t_e = on_act([t_e], lambda e, _, ed=ed: e.activation(
                        ed.buffer[:], ed.buffer[:], ACT.Exp, scale=-1.0))
                    t_m = on_dve([t_e, t_gt], lambda e, _, ed=ed: e.tensor_tensor(
                        by_head(ed.buffer[:], P), by_head(ed.buffer[:], P),
                        gt[:, c, :].unsqueeze(1).to_broadcast([P, hpg, P]), ALU.mult))
                    out_.append((ed, md, t_m, m_free))
                rhs.done(t_a)
                made = []
                for ed, md, t_m, m_free in out_:
                    t_hi = on_act([t_m, m_free], lambda e, _, ed=ed, md=md: e.mul(
                        md.buffer[:, 0, :], ed.buffer[:], M_SCALE))
                    made.append((md, on_dve([t_hi, m_free], lambda e, _, ed=ed, md=md: e.scalar_tensor_tensor(
                        out=md.buffer[:, 1, :], in0=ed.buffer[:], scalar=M_SCALE, in1=md.buffer[:, 0, :],
                        op0=ALU.mult, op1=ALU.subtract))))
                    ed.done(made[-1][1])
                return made, t_a

            def before_chunk(u):
                c, hf = units[u]
                b, h0, bo = c // (chunks // batches), hf * hph, banks[5]
                st = state[b][:, hf * half:(hf + 1) * half]
                free = bo.take()
                t_o = on_pe([free, state_ready[b][hf]], lambda e, _: e.matmul(
                    bo.buffer[:], ct[:, c * P:(c + 1) * P], st, start=True, stop=True))
                t_sd = on_pool([t_o, decays], lambda e, _: e.tensor_tensor(
                    by_head(st, hd), by_head(st, hd),
                    heads_over(sml["dec"][:, c, :], h0, hph, hd), ALU.mult))
                y_ = yac[u % 2]
                y_free = y_.take()
                t_1 = on_dve([t_o, decays, y_free], lambda e, _: e.tensor_tensor(
                    by_head(y_.buffer[:], hd), by_head(bo.buffer[:], hd),
                    heads_over(sml["ecs"][:, c, :], h0, hph, hd), ALU.mult))
                bo.done(t_1)
                return st, t_sd, y_, t_1

            def scan(u, mats, from_state):
                c, hf = units[u]
                b = c // (chunks // batches)
                st, t_sd, y_, t_1 = from_state
                x_, _, t_sk, t_xe, t_xp = xes[u]
                g_, t_gz = gates[u]
                by, bs = banks[4], banks[6]
                free = by.take()
                for h in range(hph):
                    md, t_m = mats[h // hpg]
                    for n, (a, v_) in enumerate(split_passes([md.buffer[:, q, :] for q in range(2)], xdp)):
                        t_y = on_pe([free, t_m, t_xp], lambda e, _, h=h, a=a, v_=v_, n=n: e.matmul(
                            by.buffer[:, h * hd:(h + 1) * hd], a[:, (h % hpg) * P:(h % hpg + 1) * P],
                            v_[:, h * hd:(h + 1) * hd], start=(n == 0), stop=(n == 2)),
                            mark=(h % hpg == hpg - 1 and n == 2))
                    if h % hpg == hpg - 1:
                        md.done(t_y)
                xdp_s.done(t_y)
                free = bs.take()
                t_s = on_pe([free, t_xe, t_bk], lambda e, _: e.matmul(
                    bs.buffer[:], btok[:, c * P:(c + 1) * P], xst.buffer[:], start=True, stop=True))
                xst.done(t_s)
                t_2 = on_pool([t_1, t_sk], lambda e, _: e.tensor_tensor(
                    y_.buffer[:], y_.buffer[:], x_.buffer[:], ALU.add))
                x_.done(t_2)
                t_3 = on_dve([t_2, t_y], lambda e, _: e.scalar_tensor_tensor(
                    out=y_.buffer[:], in0=by.buffer[:], scalar=1.0 / (M_SCALE * XDT_SCALE),
                    in1=y_.buffer[:], op0=ALU.mult, op1=ALU.add))
                by.done(t_3)
                t_sa = on_dve([t_sd, t_s], lambda e, _: e.tensor_tensor(st, bs.buffer[:], st, ALU.add))
                bs.done(t_sa)
                state_ready[b][hf] = [t_sa]
                t_4 = on_dve([t_3, t_gz], lambda e, _: e.tensor_tensor(
                    y_.buffer[:], y_.buffer[:], g_.buffer[:], ALU.mult))
                g_.done(t_4)
                return t_4, y_, (t_y, t_s)

            y_parts = {}

            def turn_y(u, t_4, y_):
                c, hf = units[u]
                bk = banks[7]
                free = bk.take()
                per = half // P
                for j in range(per):
                    t_t = on_pe([free, t_4], lambda e, _, j=j: e.transpose(
                        bk.buffer[:, j * P:(j + 1) * P], y_.buffer[:, j * P:(j + 1) * P], idn[:]),
                        mark=(j == per - 1))
                y_.done(t_t)
                ks = slice(hf * per, (hf + 1) * per)
                if hf == 0:
                    y_parts["free"], y_parts["ready"] = yt_s.take(), []
                src = bk.buffer[:].rearrange("p (k t) -> p k t", k=per)
                down = Y_SCALE / (2.0 * XN_SCALE * W_SCALE)
                t_hi = on_act([t_t, y_parts["free"]], lambda e, _: e.mul(yt[0][:, ks, :], src, down))
                t_lo = on_dve([t_hi, y_parts["free"]], lambda e, _: e.scalar_tensor_tensor(
                    out=yt[1][:, ks, :], in0=src, scalar=down, in1=yt[0][:, ks, :],
                    op0=ALU.mult, op1=ALU.subtract))
                bk.done(t_hi, t_lo)
                y_parts["ready"] += [t_hi, t_lo]

            attn = {}

            def project_out(c):
                bk = banks[7]
                free = bk.take()
                y_ready = y_parts["ready"]
                n = 0
                for k in range(ki):
                    for a, b in split_passes(yt, wo):
                        n += 1
                        t_p = on_pe([free, y_ready] if n == 1 else [], lambda e, _, k=k, a=a, b=b, n=n: e.matmul(
                            bk.buffer[:], a[:, k, :], b[:, k, :], start=(n == 1), stop=(n == 3 * ki)),
                            mark=(n == 3 * ki))
                yt_s.done(t_p)
                r = res[c]
                free = r.take()
                landed = load([free], lambda e, blk: e.dma_start(r.buffer[:], rows(x, c, blk)), st_res[c])
                t_r = on_dve([t_p, landed], lambda e, _: e.scalar_tensor_tensor(
                    out=r.buffer[:], in0=bk.buffer[:], scalar=1.0 / (Y_SCALE * W_SCALE), in1=r.buffer[:],
                    op0=ALU.mult, op1=ALU.add))
                bk.done(t_r)
                attn[c] = t_r

            state_ready = [[[made["state", b, hf]] for hf in range(halves)] for b in range(batches)]
            spread_heads(0)
            spread_heads(1)
            project_x(0)
            mats, t_arg = decay(0)
            project_z(1)
            spread_heads(2)
            done_y = None
            for u in range(len(units)):
                here = mats
                old = before_chunk(u)
                aside(beside[u][0])
                if u:
                    turn_y(*done_y)
                if u + 1 < len(units):
                    mats, t_arg = decay(u + 1)
                aside(beside[u][1])
                t_4, y_, t_scan = scan(u, here, old)
                aside(beside[u][2])
                done_y = (u, t_4, y_)
                if u + 1 < len(units):
                    project_x(u + 1)
                aside(beside[u][3])
                if u == 2:
                    weights_ready("w_out")
                if u and units[u - 1][1] == halves - 1:
                    project_out(units[u - 1][0])
                if u + 2 < len(units):
                    project_z(u + 2)
                spread_heads(u + 3)
            small_s.done(t_4, t_scan[0], t_arg)
            gt_s.done(t_4)
            for b in range(batches):
                for hf in range(halves):
                    made["state", b, hf] = state_ready[b][hf][0]
            arena_s.done(xes[len(units) - 1][1])
            arena_b.done(*t_scan)

            s_free, b_free = arena_s.take(), arena_b.take()
            h_ready, mids = [], {}

            def ffn_up(m):
                ts = []
                for j in range(2):
                    bk = banks[2 * (m % 2) + j]
                    free = bk.take()
                    n = 0
                    for k in range(kd):
                        for part in xt:
                            n += 1
                            t = on_pe([free], lambda e, _, j=j, k=k, part=part, bk=bk, n=n: e.matmul(
                                bk.buffer[:], q12[:, j, k, m * P:(m + 1) * P], part[:, k, :],
                                start=(n == 1), stop=(n == 2 * kd)), mark=(n == 2 * kd), apart=True)
                    ts.append((t, bk))
                (t_1, b1), (t_2, b2) = ts
                th, fl = tnh[m % 2], full[m % 2]
                th_free, fl_free = th.take(), fl.take()
                t_th = on_act([t_1, th_free], lambda e, _: e.activation(
                    th.buffer[:], b1.buffer[:], ACT.Tanh, scale=0.5 / XN_SCALE))
                b1.done(t_th)
                t_f = on_dve([t_th, t_2, fl_free], lambda e, _: e.scalar_tensor_tensor(
                    out=fl.buffer[:], in0=th.buffer[:], scalar=1.0, in1=b2.buffer[:],
                    op0=ALU.add, op1=ALU.mult))
                b2.done(t_f)
                th.done(t_f)
                mids[m] = (fl, t_f)
                return t_2

            def ffn_parts(m):
                fl, t_f = mids[m]
                hid_free = [s_free, b_free if (m + 1) * 2 * tb > after_s else []]
                hid_free = hid_free[0] + hid_free[1]
                t_hi = on_act([t_f, hid_free], lambda e, _: e.copy(hid[:, m, 0, :], fl.buffer[:]))
                t_lo = on_dve([t_hi, hid_free], lambda e, _: e.tensor_tensor(
                    hid[:, m, 1, :], fl.buffer[:], hid[:, m, 0, :], ALU.subtract))
                fl.done(t_lo)
                h_ready.append(t_lo)

            weights_ready("w1, w2")
            between, x_tok = ([], []) if last else norm(1)
            for m in range(kf):
                if m:
                    ffn_parts(m - 1)
                t_2 = ffn_up(m)
                if m >= 1:
                    aside(1)
                if m == 0:
                    turn_y(*done_y)
                if m == 1:
                    project_out(units[-1][0])
                if m >= 1 and between:
                    between.pop(0)()
            while between:
                between.pop(0)()
            if not last:
                made["xt"] = turn(x_tok, t_2)
            ffn_parts(kf - 1)

            behind = []

            def next_branch(m):
                if m < ki:
                    behind.append((m, *x_branch(m, made["xt"])))
                if m:
                    silu(*behind.pop(0))

            following = [] if last else [[0], [1], [2], [3, 4], [5], [6, 7], [], []]
            weights_ready("w3")
            for c in range(chunks):
                bk = banks[c]
                free = bk.take()
                n = 0
                for m in range(kf):
                    if m == kf // 2 and not last:
                        for tile in following[2 * c]:
                            next_branch(tile)
                    for p in range(2):
                        n += 1
                        t_p = on_pe([free, h_ready[m]], lambda e, _, m=m, p=p, c=c, bk=bk, n=n: e.matmul(
                            bk.buffer[:], hid[:, m, p, c * P:(c + 1) * P], q3[:, m, :],
                            start=(n == 1), stop=(n == 2 * kf)), mark=(n == 2 * kf), apart=True)
                r = res[c]
                t_r = on_dve([t_p, attn[c]], lambda e, _, r=r, bk=bk: e.scalar_tensor_tensor(
                    out=r.buffer[:], in0=bk.buffer[:], scalar=1.0 / HID_SCALE, in1=r.buffer[:],
                    op0=ALU.mult, op1=ALU.add))
                bk.done(t_r)
                stored = load([t_r], lambda e, blk, r=r, c=c: e.dma_start(rows(out, c, blk), r.buffer[:]), st_out[c])
                r.done(stored)
                if not last:
                    for tile in following[2 * c + 1]:
                        next_branch(tile)
            if not last:
                next_branch(ki)
            arena_s.done(t_p)
            arena_b.done(t_p)

        st_ident, st_taps, st_small = (stream(n, DMA) for n in ("ident", "taps", "small"))
        t_idn = load([], lambda e, _: e.dma_start(idn[:], ident), st_ident)
        t_half = on_pool([], lambda e, _: e.memset(mhalf[:], -0.5))
        steps, x_tok = norm(0, [t_half])
        for step in steps:
            step()
        wdt = sb("wdt", [heads, heads])
        for dst, src in ((cw, conv_w), (cb, conv_b), (wdt, w_dt)):
            t_taps = load([], lambda e, _, dst=dst, src=src: e.dma_start(dst[:], src), st_taps)
        t_clear = [on_pool([], lambda e, _, b=b: e.memset(state[b][:], 0.0)) for b in range(batches)]
        t_clear.append(on_pool([], lambda e, _: e.memset(hal[:], 0.0)))
        t_one = on_pool([], lambda e, _: e.memset(ones[:], 1.0))
        for b in range(batches):
            for hf in range(halves):
                made["state", b, hf] = t_clear[b]

        width = w_x.shape[1]
        stage = [(arena[:, 2 * n * width:2 * (n + 1) * width].bitcast(F32), Slot(pr), stream(f"stage{n}", DMA))
                 for n in range(4)]
        st_stage = [st for _, _, st in stage]
        arena_s.take()
        arena_b.take()
        turns = {}

        def next_in(ring):
            first_stream = ring[0][2]
            turns[first_stream] = turns.get(first_stream, 0) + 1
            return ring[(turns[first_stream] - 1) % len(ring)]

        def split(ring, src, hi, lo):
            buf, s, st = next_in(ring)
            buf = buf[:, 0:src.shape[1]]
            landed = load(s.take(), lambda e, _: e.dma_start(buf, src), st)
            t_hi = on_act([landed], lambda e, _: e.activation(hi, buf, ACT.Copy, scale=W_SCALE))

            def rest():
                t_lo = on_dve([landed, t_hi], lambda e, _: e.scalar_tensor_tensor(
                    out=lo, in0=buf, scalar=W_SCALE, in1=hi, op0=ALU.mult, op1=ALU.subtract))
                s.done(t_hi, t_lo)
                return t_lo

            return rest

        pieces = []
        for cols in (slice(0, di), slice(di, 2 * di)):
            for k in range(kd):
                pieces.append((w_in[k * P:(k + 1) * P, cols], win[0][:, k, cols], win[1][:, k, cols]))
        for n in range(kd):
            t_win = split(stage, *pieces[n])()
        made["xt"] = turn(x_tok, [])
        for n in range(kd, 2 * kd):
            t_win_z = split(stage, *pieces[n])()

        t_cws = on_dve([t_taps], lambda e, _: e.tensor_scalar(
            cws[:], cw[:, :, taps - 1], CONV_SCALE / (XN_SCALE * W_SCALE), None, ALU.mult))
        t_cw = on_dve([t_cws], lambda e, _: e.tensor_scalar(cw[:], cw[:], CONV_SCALE, None, ALU.mult))
        t_cb = on_dve([t_taps], lambda e, _: e.tensor_scalar(cb[:], cb[:], CONV_SCALE, None, ALU.mult))
        for dst, src in ((upp, upper), (csr, cs_rows), (csh, cs_heads)):
            t_small = load([], lambda e, _, dst=dst, src=src: e.dma_start(dst[:], src), st_small)
        for dst, src in ((dtb, dt_bias), (na, a_log), (dsk, d_skip)):
            t_small = load([], lambda e, _, dst=dst, src=src: e.dma_start(
                dst[:], src.unsqueeze(0).to_broadcast([P, heads])), st_small)
        free = full[0].take() + full[1].take()
        for n in range(halves):
            t_small = load(free, lambda e, _, n=n: e.dma_start(
                full[n].buffer[0:heads, :], w_xdt[:, n * half:(n + 1) * half]), st_small)
        for name in ("scalar", "vector"):
            pr.step(name, [t_taps, t_cws, t_cw, t_cb], None)
        pr.step("tensor", [t_win], None)
        behind = []
        for m in range(ki + 1):
            if m < ki:
                behind.append((m, *x_branch(m, made["xt"], t_clear)))
                t_wx = split(stage, w_x[m * P:(m + 1) * P, :], wx[0][:, m, :], wx[1][:, m, :])()
            if m:
                silu(*behind.pop(0))
            if m == 2:
                free = banks[1].take()
                per = half // P
                for k in range(ki):
                    t_w2 = on_pe([t_taps, t_small, free], lambda e, _, k=k: e.matmul(
                        banks[1].buffer[:, k * heads:(k + 1) * heads],
                        full[k // per].buffer[0:heads, k % per * P:(k % per + 1) * P], wdt[:],
                        start=True, stop=True))
                full[0].done(t_w2)
                full[1].done(t_w2)
                flat = [w[:].rearrange("p k h -> p (k h)") for w in w2]
                t_hi = on_act([t_w2], lambda e, _: e.activation(
                    flat[0], banks[1].buffer[:, 0:ki * heads], ACT.Copy, scale=W_SCALE))
                t_w2 = on_dve([t_hi], lambda e, _: e.scalar_tensor_tensor(
                    out=flat[1], in0=banks[1].buffer[:, 0:ki * heads], scalar=W_SCALE, in1=flat[0],
                    op0=ALU.mult, op1=ALU.subtract))
                banks[1].done(t_hi, t_w2)
                t_exp = on_act([t_small], lambda e, _: e.activation(na[:], na[:], ACT.Exp))
                t_na = on_dve([t_exp], lambda e, _: e.tensor_scalar(na[:], na[:], -1.0, None, ALU.mult))
        arena_s.done(*[t for _, s, _ in stage for t in s.readers])
        arena_b.done(*[t for _, s, _ in stage for t in s.readers])
        for name in ("tensor", "scalar", "vector", "gpsimd"):
            pr.step(name, [t_small, t_na, t_one], None)
        pr.step("tensor", [t_win_z], None)
        prepared = {"w_x": [t_wx, t_w2]}

        fcols = kd * fh
        pieces_per = fcols // half
        asum = sb("asum", [P, 3, pieces_per])
        tsum, gam, rgam = (sb(n, [P, 3]) for n in ("tsum", "gam", "rgam"))
        assert fcols % half == 0
        early_ring = [(r.buffer[:], r, stream(f"early{n}", DMA)) for n, r in enumerate(res)]
        late_ring = [(r.buffer[:], r, stream(f"late{n}", DMA)) for n, r in enumerate((*full, res[3]))]
        ffn_ring = [(r.buffer[:], r, stream(f"beside_ffn{n}", DMA)) for n, r in enumerate((*edc, *xs))]
        beside_ffn = kf - 2

        def magnitudes(n):
            j, i = divmod(n, pieces_per)
            buf, s, st = next_in(early_ring)
            landed = load(s.take(), lambda e, _: e.dma_start(
                buf, w_ffn[:, n * half:(n + 1) * half]), st)
            t = on_act([landed], lambda e, _: e.activation(
                buf, buf, ACT.Abs, accum_out=asum[:, j, i:i + 1]))
            s.done(t)
            prepared["sums"] = t

        def sums():
            prepared["sums"] = on_dve([prepared["sums"]], lambda e, _: e.reduce_sum(
                tsum[:], asum[:], mybir.AxisListType.X))

        def scales():
            free = banks[7].take()
            t = on_pe([prepared["sums"], free], lambda e, _: e.matmul(
                banks[7].buffer[:, 0:3], ones[:], tsum[:], start=True, stop=True))
            t = on_dve([t], lambda e, _: e.tensor_scalar(
                gam[:], banks[7].buffer[:, 0:3], 1.0 / (dm * fh), 1e-8, ALU.mult, ALU.add))
            banks[7].done(t)
            prepared["1 / gamma"] = on_dve([t], lambda e, _: e.reciprocal(rgam[:], gam[:]))

        q_flat = [q12[:, 0].rearrange("p k n -> p (k n)"), q12[:, 1].rearrange("p k n -> p (k n)"),
                  q3[:].rearrange("p k n -> p (k n)")]

        def ternary(n):
            j, i = divmod(n, pieces_per)
            buf, s, st = next_in(late_ring if n < n_ff - beside_ffn else ffn_ring)
            landed = load(s.take(), lambda e, _: e.dma_start(
                buf, w_ffn[:, n * half:(n + 1) * half]), st)
            t = on_dve([prepared["1 / gamma"], landed], lambda e, _: e.tensor_scalar(
                buf, buf, rgam[:, j:j + 1], ROUND, ALU.mult, ALU.add))
            t = on_dve([t], lambda e, _: e.tensor_scalar(
                buf, buf, ROUND + 1.0, ROUND - 1.0, ALU.min, ALU.max))

            def rest():
                t_q = on_act([t], lambda e, _: e.activation(
                    q_flat[j][:, i * half:(i + 1) * half], buf, ACT.Copy, bias=-ROUND, saturate=False))
                s.done(t_q)
                prepared["w3" if j == 2 else "w1, w2"] = [t_q]

            return rest

        def out_weights(k):
            rest = split(early_ring, w_out[k * P:(k + 1) * P, :], wo[0][:, k, :], wo[1][:, k, :])

            def finish():
                prepared["w_out"] = [rest()]

            return finish

        n_ff = 3 * pieces_per
        at_start = 12
        preparation = [lambda n=n: magnitudes(n) for n in range(at_start)]
        preparation += [lambda k=k: out_weights(k) for k in range(ki)]
        preparation += [lambda n=n: magnitudes(n) for n in range(at_start, n_ff)]
        preparation += [sums, scales]
        preparation += [lambda n=n: ternary(n) for n in range(n_ff - beside_ffn)] + [lambda: None]
        preparation += [lambda n=n: ternary(n) for n in range(n_ff - beside_ffn, n_ff)] + [lambda: None]
        after = [None]
        beside = [[3, 3, 3, 3], [3, 3, 3, 3], [2, 2, 1, 1], [1, 2, 2, 1],
                  [2, 1, 1, 1], [2, 1, 1, 1], [2, 1, 1, 1], [2, 1, 1, 1]]
        assert sum(map(sum, beside)) + at_start + kf - 1 == len(preparation)

        pr.section = "first"
        body(True, False)
        assert not preparation
        pr.section = "loop"
        body(False, False)
        pr.section = "last"
        body(False, True)
        for s in streams:
            assert s.counts["first"] == s.counts["loop"]
        finals = [Token(s, "last", s.counts["last"]) for s in st_out]
        pr.step("sync", finals, None)

        block = ctx.enter_context(nc.Block())

        def emit(name):
            def run(eng):
                pr.play(name, eng, "setup", 0)
                pr.play(name, eng, "first", 0)
                with eng.Fori(1, nb - 1) as i:
                    pr.play(name, eng, "loop", i)
                pr.play(name, eng, "last", nb - 1)
            return run

        block.tensor(emit("tensor"))
        block.scalar(emit("scalar"))
        block.vector(emit("vector"))
        block.gpsimd(emit("gpsimd"))
        block.sync(emit("sync"))


def kernel(**inputs):
    import concourse.bacc as bacc
    from concourse.bass_utils import run_bass_kernel_spmd

    def get(name):
        return np.asarray(inputs[name])

    def tiles(w):
        n, k = w.shape
        return np.ascontiguousarray(w.T.reshape(k // P, P, n).transpose(1, 0, 2).reshape(P, -1))

    heads = 16
    w_x = get("L0_attn_x_proj_w")
    di = w_x.shape[1]
    cw = get("L0_attn_conv_w")
    ki = cw.shape[0] // P
    bf16 = np.dtype("bfloat16")
    s_, l_ = np.arange(P)[:, None], np.arange(P)[None, :]
    upper = (s_ <= l_).astype(np.float32)
    row = np.arange(6 * heads)
    part, second = row // heads % 3, row >= 3 * heads
    cs_rows = np.stack([part == 0, part == 1, part == 2, -1.0 * ~second, second, second, ~second],
                       axis=1).astype(np.float32)
    cs_heads = (row[:, None] % heads == np.arange(heads)).astype(bf16)
    arrays = {
        "x": get("L0_attn_x"),
        "w_in": np.ascontiguousarray(get("L0_attn_in_proj_w").T),
        "conv_w": np.ascontiguousarray(cw.reshape(ki, P, -1).transpose(1, 0, 2)),
        "conv_b": np.ascontiguousarray(get("L0_attn_conv_b").reshape(ki, P).T),
        "w_x": np.ascontiguousarray(np.concatenate([w_x[:di], w_x[di + heads:]]).T),
        "w_xdt": np.ascontiguousarray(w_x[di:di + heads]),
        "w_dt": np.ascontiguousarray(get("L0_attn_dt_proj_w").T),
        "dt_bias": get("L0_attn_dt_proj_b"),
        "a_log": get("L0_attn_A_log"),
        "d_skip": get("L0_attn_D"),
        "w_out": np.ascontiguousarray(get("L0_attn_out_proj_w").T),
        "w_ffn": np.concatenate([tiles(get(f"L0_ffn_w{n}")) for n in (1, 2, 3)], axis=1),
        "ident": np.eye(P, dtype=np.float32),
        "upper": upper,
        "cs_rows": cs_rows,
        "cs_heads": cs_heads,
    }
    nc = bacc.Bacc("TRN2", target_bir_lowering=False, num_devices=1, dynamic_dma_scratch_size=1024)
    args = [nc.dram_tensor(n, a.shape, mybir.dt.from_np(a.dtype), kind="ExternalInput").ap()
            for n, a in arrays.items()]
    out = nc.dram_tensor("out", arrays["x"].shape, F32, kind="ExternalOutput").ap()
    mamba_ffn_block(nc, *args, out)
    return run_bass_kernel_spmd(nc, [arrays], core_ids=[0]).results[0]["out"]
```
